# Optimizing a Trainium2 kernel written in Bass

```python
import numpy as np
import jax
import jax.numpy as jnp

def _softmax(x, axis=-1):
    return jax.nn.softmax(x, axis=axis)

def _gelu(x):
    return jax.nn.gelu(x, approximate=True)

def _silu(x):
    return jax.nn.silu(x)

def _sigmoid(x):
    return jax.nn.sigmoid(x)

def _layernorm(x, axis=-1, eps=1e-05):
    m = jnp.mean(x, axis=axis, keepdims=True)
    v = jnp.var(x, axis=axis, keepdims=True)
    return (x - m) / jnp.sqrt(v + eps)

def _scatter_add(tgt, idx, src, axis=0):
    return tgt.at[idx].add(src)

def _segment_sum(src, seg, n):
    return jax.ops.segment_sum(src, seg, n)
kernel_name = 'mk_lm_tower_d1_tok_ids2048_r4_805055'

def setup_inputs(seed: int=0):
    np.random.seed(seed)
    _w = jnp.asarray

    def _rec_inputs():
        import jax
        import jax.numpy as jnp
        _rk = jax.random.key(seed)
        x = jax.random.randint(jax.random.fold_in(_rk, 1), (8, 1024), 0, 127999, jnp.int32)
        return x
    x = _rec_inputs()

    def _L0_tok_setup():
        import jax, jax.numpy as jnp
        import numpy as np
        VOCAB = 32000
        DIM = 512
        RANK = 16
        ALPHA = 16.0
        SCALING = ALPHA / RANK
        key = jax.random.key(seed)
        k1, k2, k3, k4 = jax.random.split(key, 4)
        x = jax.random.randint(k1, (8, 1024), 0, VOCAB, dtype=jnp.int64 if jax.config.jax_enable_x64 else jnp.int32)
        W = jax.random.normal(k2, (VOCAB, DIM), dtype=jnp.float32)
        A = jax.random.normal(k3, (VOCAB, RANK), dtype=jnp.float32)
        B = jax.random.normal(k4, (RANK, DIM), dtype=jnp.float32)
        return {'x': x, 'W': W, 'A': A, 'B': B}
    _L0_tok_all = _L0_tok_setup()
    _L0_tok_in = {k: v for k, v in _L0_tok_all.items() if k in ('W', 'A', 'B')}
    del _L0_tok_all

    def _L0_attn_setup():
        import jax, jax.numpy as jnp
        import numpy as np
        HID = 512
        NH = 32
        DK = 256
        DV = 512
        HQK = DK // NH
        HV = DV // NH
        RLO = 32
        GLO = 64
        EPS = 1e-05
        B, L = (4, 1024)

        def _forward(x, mu_x, Wx1, Wx2, Wr, Ww1, Ww2, bw, Wk, Wv, Wg, bonus, gn_w, gn_b, Wo):
            Bn, Ln, _ = x.shape
            delta = jnp.pad(x[:, :-1], ((0, 0), (1, 0), (0, 0))) - x
            z = jnp.tanh((x + delta * mu_x) @ Wx1).reshape(Bn, Ln, 5, RLO)
            mus = jnp.einsum('blnr,nrd->blnd', z, Wx2)
            mr, mw, mk, mv, mg = (mus[:, :, i] for i in range(5))
            r = (x + delta * mr) @ Wr
            w = jnp.tanh((x + delta * mw) @ Ww1) @ Ww2 + bw
            k = (x + delta * mk) @ Wk
            v = (x + delta * mv) @ Wv
            g = (x + delta * mg) @ Wg
            heads = lambda t, d: t.reshape(Bn, Ln, NH, d).transpose(1, 0, 2, 3)
            r_t, k_t = (heads(r, HQK), heads(k, HQK))
            v_t = heads(v, HV)
            decay = jnp.exp(-jnp.exp(heads(w, HQK)))

            def step(S, inp):
                rt, kt, vt, dt = inp
                kv = kt[..., :, None] * vt[..., None, :]
                ot = jnp.einsum('bhk,bhkv->bhv', rt, S + bonus[None, :, :, None] * kv)
                return (S * dt[..., :, None] + kv, ot)
            S0 = jnp.zeros((Bn, NH, HQK, HV), x.dtype)
            _, o = jax.lax.scan(step, S0, (r_t, k_t, v_t, decay))
            o = o.transpose(1, 0, 2, 3)
            mean = o.mean(-1, keepdims=True)
            var = o.var(-1, keepdims=True)
            on = (o - mean) * jax.lax.rsqrt(var + EPS) * gn_w + gn_b
            gh = g.reshape(Bn, Ln, NH, HV)
            o = on * (gh * jax.nn.sigmoid(gh))
            return o.reshape(Bn, Ln, DV) @ Wo
        key = jax.random.key(seed)
        ks = jax.random.split(key, 16)
        s = 0.02
        return {'hidden_states': jax.random.normal(ks[0], (B, L, HID), jnp.float32), 'mu_x': jax.random.uniform(ks[1], (HID,), jnp.float32), 'Wx1': jax.random.normal(ks[2], (HID, 5 * RLO), jnp.float32) * s, 'Wx2': jax.random.normal(ks[3], (5, RLO, HID), jnp.float32) * s, 'Wr': jax.random.normal(ks[4], (HID, DK), jnp.float32) * s, 'Ww1': jax.random.normal(ks[5], (HID, GLO), jnp.float32) * s, 'Ww2': jax.random.normal(ks[6], (GLO, DK), jnp.float32) * s, 'bw': jnp.zeros((DK,), jnp.float32), 'Wk': jax.random.normal(ks[7], (HID, DK), jnp.float32) * s, 'Wv': jax.random.normal(ks[8], (HID, DV), jnp.float32) * s, 'Wg': jax.random.normal(ks[9], (HID, DV), jnp.float32) * s, 'bonus': jax.random.normal(ks[10], (NH, HQK), jnp.float32) * s, 'gn_w': jnp.ones((HV,), jnp.float32), 'gn_b': jnp.zeros((HV,), jnp.float32), 'Wo': jax.random.normal(ks[11], (DV, HID), jnp.float32) * s}
    _L0_attn_all = _L0_attn_setup()
    _L0_attn_in = {k: v for k, v in _L0_attn_all.items() if k in ('mu_x', 'Wx1', 'Wx2', 'Wr', 'Ww1', 'Ww2', 'bw', 'Wk', 'Wv', 'Wg', 'bonus', 'gn_w', 'gn_b', 'Wo')}
    del _L0_attn_all

    def _L0_ffn_setup():
        import jax, jax.numpy as jnp
        import numpy as np

        def binarize_weight(w):
            alpha = jnp.mean(jnp.abs(w), axis=tuple(range(1, w.ndim)), keepdims=True)
            bw = jnp.where(w >= 0, 1.0, -1.0) * alpha
            return jax.lax.stop_gradient(bw - w) + w
        key = jax.random.key(seed)
        k1, k2, k3 = jax.random.split(key, 3)
        in_features, out_features = (512, 512)
        x = jax.random.normal(k1, (8, 512, in_features), dtype=jnp.float32)
        std = np.sqrt(2.0 / out_features).astype(np.float32)
        weight = jax.random.normal(k2, (out_features, in_features), dtype=jnp.float32) * std
        bias = jax.random.normal(k3, (out_features,), dtype=jnp.float32) * 0.01
        return {'x': x, 'weight': weight, 'bias': bias}
    _L0_ffn_all = _L0_ffn_setup()
    _L0_ffn_in = {k: v for k, v in _L0_ffn_all.items() if k in ('weight', 'bias')}
    del _L0_ffn_all
    return {'x': x, 'L0_tok_W': _L0_tok_in['W'], 'L0_tok_A': _L0_tok_in['A'], 'L0_tok_B': _L0_tok_in['B'], 'L0_attn_mu_x': _L0_attn_in['mu_x'], 'L0_attn_Wx1': _L0_attn_in['Wx1'], 'L0_attn_Wx2': _L0_attn_in['Wx2'], 'L0_attn_Wr': _L0_attn_in['Wr'], 'L0_attn_Ww1': _L0_attn_in['Ww1'], 'L0_attn_Ww2': _L0_attn_in['Ww2'], 'L0_attn_bw': _L0_attn_in['bw'], 'L0_attn_Wk': _L0_attn_in['Wk'], 'L0_attn_Wv': _L0_attn_in['Wv'], 'L0_attn_Wg': _L0_attn_in['Wg'], 'L0_attn_bonus': _L0_attn_in['bonus'], 'L0_attn_gn_w': _L0_attn_in['gn_w'], 'L0_attn_gn_b': _L0_attn_in['gn_b'], 'L0_attn_Wo': _L0_attn_in['Wo'], 'L0_ffn_weight': _L0_ffn_in['weight'], 'L0_ffn_bias': _L0_ffn_in['bias']}

def reference(x, L0_tok_W, L0_tok_A, L0_tok_B, L0_attn_mu_x, L0_attn_Wx1, L0_attn_Wx2, L0_attn_Wr, L0_attn_Ww1, L0_attn_Ww2, L0_attn_bw, L0_attn_Wk, L0_attn_Wv, L0_attn_Wg, L0_attn_bonus, L0_attn_gn_w, L0_attn_gn_b, L0_attn_Wo, L0_ffn_weight, L0_ffn_bias):
    import jax
    import jax.numpy as jnp

    def _L0_tok_ref(x, W, A, B):
        import jax, jax.numpy as jnp
        import numpy as np
        VOCAB = 32000
        DIM = 512
        RANK = 16
        ALPHA = 16.0
        SCALING = ALPHA / RANK
        base = W[x]
        after_A = A[x]
        lora_out = jnp.einsum('bsr,rd->bsd', after_A, B)
        return base + lora_out * SCALING

    def _L0_attn_ref(hidden_states, mu_x, Wx1, Wx2, Wr, Ww1, Ww2, bw, Wk, Wv, Wg, bonus, gn_w, gn_b, Wo):
        import jax, jax.numpy as jnp
        import numpy as np
        HID = 512
        NH = 32
        DK = 256
        DV = 512
        HQK = DK // NH
        HV = DV // NH
        RLO = 32
        GLO = 64
        EPS = 1e-05
        B, L = (4, 1024)

        def _forward(x, mu_x, Wx1, Wx2, Wr, Ww1, Ww2, bw, Wk, Wv, Wg, bonus, gn_w, gn_b, Wo):
            Bn, Ln, _ = x.shape
            delta = jnp.pad(x[:, :-1], ((0, 0), (1, 0), (0, 0))) - x
            z = jnp.tanh((x + delta * mu_x) @ Wx1).reshape(Bn, Ln, 5, RLO)
            mus = jnp.einsum('blnr,nrd->blnd', z, Wx2)
            mr, mw, mk, mv, mg = (mus[:, :, i] for i in range(5))
            r = (x + delta * mr) @ Wr
            w = jnp.tanh((x + delta * mw) @ Ww1) @ Ww2 + bw
            k = (x + delta * mk) @ Wk
            v = (x + delta * mv) @ Wv
            g = (x + delta * mg) @ Wg
            heads = lambda t, d: t.reshape(Bn, Ln, NH, d).transpose(1, 0, 2, 3)
            r_t, k_t = (heads(r, HQK), heads(k, HQK))
            v_t = heads(v, HV)
            decay = jnp.exp(-jnp.exp(heads(w, HQK)))

            def step(S, inp):
                rt, kt, vt, dt = inp
                kv = kt[..., :, None] * vt[..., None, :]
                ot = jnp.einsum('bhk,bhkv->bhv', rt, S + bonus[None, :, :, None] * kv)
                return (S * dt[..., :, None] + kv, ot)
            S0 = jnp.zeros((Bn, NH, HQK, HV), x.dtype)
            _, o = jax.lax.scan(step, S0, (r_t, k_t, v_t, decay))
            o = o.transpose(1, 0, 2, 3)
            mean = o.mean(-1, keepdims=True)
            var = o.var(-1, keepdims=True)
            on = (o - mean) * jax.lax.rsqrt(var + EPS) * gn_w + gn_b
            gh = g.reshape(Bn, Ln, NH, HV)
            o = on * (gh * jax.nn.sigmoid(gh))
            return o.reshape(Bn, Ln, DV) @ Wo
        return _forward(hidden_states, mu_x, Wx1, Wx2, Wr, Ww1, Ww2, bw, Wk, Wv, Wg, bonus, gn_w, gn_b, Wo)

    def _L0_ffn_ref(x, weight, bias):
        import jax, jax.numpy as jnp
        import numpy as np

        def binarize_weight(w):
            alpha = jnp.mean(jnp.abs(w), axis=tuple(range(1, w.ndim)), keepdims=True)
            bw = jnp.where(w >= 0, 1.0, -1.0) * alpha
            return jax.lax.stop_gradient(bw - w) + w
        bw = binarize_weight(weight)
        return jnp.einsum('bsi,oi->bso', x, bw) + bias
    h = _L0_tok_ref(x, L0_tok_W, L0_tok_A, L0_tok_B)
    h = h + _L0_attn_ref(_layernorm(h, axis=-1), L0_attn_mu_x, L0_attn_Wx1, L0_attn_Wx2, L0_attn_Wr, L0_attn_Ww1, L0_attn_Ww2, L0_attn_bw, L0_attn_Wk, L0_attn_Wv, L0_attn_Wg, L0_attn_bonus, L0_attn_gn_w, L0_attn_gn_b, L0_attn_Wo)
    h = h + _L0_ffn_ref(_layernorm(h, axis=-1), L0_ffn_weight, L0_ffn_bias)
    return h

_drawn_inputs = setup_inputs


def setup_inputs(seed=0):
    import zlib

    import numpy as np

    out = dict(_drawn_inputs(seed))
    spreads = {'L0_attn_bw': (0.0, 2.0), 'L0_attn_gn_w': (1.0, 0.6), 'L0_attn_gn_b': (0.0, 2.0)}
    factors = {'L0_attn_mu_x': 8.0,
     'L0_attn_Wx1': 8.0,
     'L0_attn_Wx2': 8.0,
     'L0_attn_Ww1': 8.0,
     'L0_attn_Ww2': 22.664,
     'L0_attn_bonus': 101.533,
     'L0_ffn_bias': 26.229}
    for name, (base, spread) in spreads.items():
        noise = np.random.default_rng([zlib.crc32(name.encode()), seed]).standard_normal(out[name].shape)
        drawn = base * np.exp(spread * noise) if base else spread * noise
        out[name] = jnp.asarray(drawn.astype(out[name].dtype))
    for name, factor in factors.items():
        out[name] = (out[name] * factor).astype(out[name].dtype)
    return out
```

```python
from contextlib import ExitStack

import concourse.bass as bass
from concourse import mybir

F32 = mybir.dt.float32
I32 = mybir.dt.int32
U32 = mybir.dt.uint32
ALU = mybir.AluOpType
ACT = mybir.ActivationFunctionType
AX = mybir.AxisListType

P = 128
SEQS, SEQ = 8, 1024
D = 512
KD = D // P
NH, HK, HV = 32, 8, 16
VG = 4
VT = HV // VG
HH = 2
RLO, GLO = 32, 64
RANK = 16
VOCAB = 32000
EPS = 1e-5
TB = 256
TC = TB // P
NBLK = SEQS * SEQ // TB
PER_SEQ = SEQ // TB
LOOPED = 4
VRING, KVRING, MXRING = 8, 4, 3
MIX_R, MIX_W, MIX_K, MIX_V, MIX_G = range(5)
MIXES = [MIX_W, MIX_K, MIX_V, MIX_G, MIX_R]
NC_MU, NC_U, NC_BW, NC_GW, NC_GB = 0, 4, 6, 8, 12
NW = 4

SCHEDULE = [
    ("act_xT", 0, 0), ("pe_xT", 1, 0), ("sp_spread", 15, -2), ("dv_out", 0, -3), ("gp_add", 0, -1), ("gp_kv", 15, -2),
    ("act_xT", 1, 0), ("pe_proj", 0, -1), ("pe_red", 2, -2), ("dv_scan", 15, -2), ("dv_prod", 14, -2), ("dv_prod", 15, -2),
    ("gp_bonus", 0, -2), ("dv_out", 1, -3), ("act_t2", 0, -1), ("pe_mus", 2, -1), ("dv_mus", 2, -1), ("act_store", 0, -3),
    ("gp_add", 1, -1), ("dv_mus", 3, -1), ("dv_ob", 0, -2), ("pe_red", 3, -2), ("pe_proj", 1, -1), ("dv_ob", 1, -2),
    ("pe_mean", 0, -2), ("act_k", 0, -1), ("gp_add", 2, -1), ("pe_mus", 4, -1), ("pe_pv", 0, -1), ("dv_oc", 0, -2),
    ("act_sq", 0, -2), ("act_v", 0, -1), ("pe_var", 0, -2), ("gp_gather", 0, 1), ("dv_mus", 4, -1), ("gp_add", 3, -1),
    ("pe_pv", 1, -1), ("sp_idx", 0, 3), ("act_sdo", 0, -2), ("pe_agT", 0, 1), ("pe_w2", 0, -1), ("act_v", 1, -1),
    ("act_agT", 0, 1), ("pe_lora", 0, 1), ("dv_on", 0, -2), ("act_y", 0, -2), ("dv_idx", 0, 3), ("act_ew", 0, -1),
    ("act_d", 0, -1), ("sp_spread", 0, -1), ("gp_delta", 0, 0), ("gp_add", 4, -1), ("dv_mix0", 0, 0), ("dv_lora", 0, 1),
    ("pe_lora", 1, 1), ("gp_gate", 0, -2), ("sp_spread", 1, -1), ("pe_proj", 4, -1), ("sp_spread", 2, -1), ("pe_wo", 0, -2),
    ("dv_lora", 1, 1), ("sp_spread", 3, -1), ("sp_spread", 4, -1), ("sp_spread", 5, -1), ("gp_kv", 0, -1), ("gp_kv", 1, -1),
    ("gp_kv", 2, -1), ("dv_st1", 0, 1), ("pe_wo", 1, -2), ("dv_scan", 0, -1), ("sp_spread", 6, -1), ("sp_spread", 7, -1),
    ("dv_ruk", 0, -1), ("gp_kv", 3, -1), ("pe_bs", 0, -1), ("dv_scan", 1, -1), ("dv_prod", 0, -1), ("dv_prod", 1, -1),
    ("dv_scan", 2, -1), ("gp_kv", 4, -1), ("pe_pg", 0, -1), ("dv_scan", 3, -1), ("sp_spread", 8, -1), ("dv_h2", 0, -2),
    ("pe_pg", 1, -1), ("dv_prod", 2, -1), ("act_th", 0, -1), ("dv_h2", 1, -2), ("sp_spread", 9, -1), ("gp_kv", 5, -1),
    ("gp_kv", 6, -1), ("gp_kv", 7, -1), ("dv_prod", 3, -1), ("dv_scan", 4, -1), ("dv_st2", 0, -2), ("dv_scan", 5, -1),
    ("act_sd2", 0, -2), ("pe_z", 0, 0), ("gp_kv", 8, -1), ("sp_spread", 10, -1), ("dv_scan", 6, -1), ("dv_prod", 4, -1),
    ("gp_kv", 9, -1), ("dv_scan", 7, -1), ("dv_gate", 0, -1), ("dv_prod", 5, -1), ("act_bs", 0, -1), ("dv_n2", 0, -2),
    ("dv_scan", 8, -1), ("act_sd1", 0, 1), ("gp_kv", 10, -1), ("pe_yT", 0, -2), ("sp_spread", 11, -1), ("dv_scan", 9, -1),
    ("act_th", 1, -1), ("gp_kv", 11, -1), ("sp_spread", 12, -1), ("pe_yT", 1, -2), ("act_z", 0, 0), ("dv_prod", 6, -1),
    ("dv_gate", 1, -1), ("dv_prod", 7, -1), ("dv_scan", 10, -1), ("sp_spread", 13, -1), ("act_yT", 0, -2),
    ("dv_scan", 11, -1), ("gp_kv", 12, -1), ("gp_kv", 13, -1), ("act_yT", 1, -2), ("dv_scan", 12, -1), ("dv_prod", 8, -1),
    ("pe_red", 0, -1), ("dv_n1", 0, 1), ("pe_mus", 0, 0), ("dv_mus", 0, 0), ("dv_mus", 1, 0), ("pe_red", 1, -1),
    ("gp_bias", 0, -2), ("dv_scan", 13, -1), ("sp_spread", 14, -1), ("pe_ffn", 0, -2), ("dv_prod", 9, -1),
    ("dv_prod", 10, -1), ("dv_prod", 11, -1), ("gp_kv", 14, -1), ("dv_prod", 12, -1), ("dv_scan", 14, -1),
    ("dv_prod", 13, -1), ("pe_ffn", 1, -2), ("pe_xT", 0, 1),
]
FILLS = {
    ("pe_agT", 0): ["agT"], ("pe_lora", 0): ["lora0"], ("pe_lora", 1): ["lora1"],
    ("pe_xT", 0): ["xT0"], ("pe_xT", 1): ["xT1"], ("pe_z", 0): ["z"],
    ("pe_mus", 0): ["mu0a", "mu1a", "mu0b", "mu1b"], ("pe_mus", 2): ["mu2a", "mu3a", "mu2b", "mu3b"],
    ("pe_mus", 4): ["mu4a", "mu4b"],
    ("pe_proj", 0): ["pw"], ("pe_proj", 1): ["pk"], ("pe_pv", 0): ["pv0"], ("pe_pv", 1): ["pv1"],
    ("pe_pg", 0): ["pg0"], ("pe_pg", 1): ["pg1"], ("pe_w2", 0): ["w2"], ("pe_bs", 0): ["bs"],
    ("pe_mean", 0): ["mean"], ("pe_var", 0): ["var"], ("pe_wo", 0): ["wo0"], ("pe_wo", 1): ["wo1"],
    ("pe_yT", 0): ["yT0"], ("pe_yT", 1): ["yT1"], ("pe_ffn", 0): ["f0"], ("pe_ffn", 1): ["f1"],
}


MOST, LEAST = max(x[2] for x in SCHEDULE), min(x[2] for x in SCHEDULE)
FIRST_LOOPED = 1 - LEAST


def fill_places():
    bank, per = {}, [0] * NW
    order = [(n, stage) for what, a, stage in SCHEDULE for n in FILLS.get((what, a), [])]
    for i, (n, stage) in enumerate(order):
        bank[n] = i % NW
        per[i % NW] += 1
    count, seen = {n: {} for n, _ in order}, [0] * NW
    for s in range(-MOST, NBLK - LEAST):
        for n, stage in order:
            if 0 <= s + stage < NBLK:
                seen[bank[n]] += 1
                count[n][s + stage] = seen[bank[n]]
    return bank, count, per


BANK, COUNT, PER = fill_places()
POS = {x[:2]: (i, x[2]) for i, x in enumerate(SCHEDULE)}
Y_TURNED_BEFORE = POS["dv_n2", 0][1] - POS["dv_n1", 0][1] - (POS["dv_n2", 0][0] > POS["dv_n1", 0][0])
X_TURNED_BEFORE = POS["dv_n1", 0][1] - POS["dv_n2", 0][1] - (POS["dv_n1", 0][0] > POS["dv_n2", 0][0])


class Block:

    def __init__(self, off, turn=None):
        self.off, self.turn = off, turn

    def __add__(self, n):
        return Block(self.off + n, self.turn)

    def times(self, per, c=0):
        const = per * self.off + c
        if self.turn is None:
            return const
        assert const > 0
        return self.turn * (per * LOOPED) + const

    def round(self, n, per, c=0):
        const = per * (self.off // n) + c
        if self.turn is None:
            return const
        assert const > 0
        return self.turn * (per * (LOOPED // n)) + const

    def fill(self, name, c=0):
        const = COUNT[name][self.off] + c
        if self.turn is None:
            return const
        per = PER[BANK[name]] * LOOPED
        assert const > 0 and COUNT[name][self.off + LOOPED] + c - const == per
        return self.turn * per + const


def wait(eng, sem, value):
    if isinstance(value, int) and value <= 0:
        return
    eng.wait_ge(sem, value)


def whole_run(eng, pieces):
    def step(off, turn=None):
        for what, a, stage in SCHEDULE:
            b = off + stage
            if what in pieces and (turn is not None or 0 <= b < NBLK):
                pieces[what](Block(b, turn), a)

    turns = (NBLK - MOST - FIRST_LOOPED) // LOOPED
    for s in range(-MOST, FIRST_LOOPED):
        step(s)
    with eng.Fori(0, turns) as turn:
        for u in range(LOOPED):
            step(FIRST_LOOPED + u, turn)
    for s in range(FIRST_LOOPED + turns * LOOPED, NBLK - LEAST):
        step(s)


def tower_kernel(nc, x, w_tok, a_tok, b_tok, vecs, wx1, wx2, wr, ww1, ww2, wk, wv, wg, wo, w_ffn, b_ffn, out):
    ctx = ExitStack()
    with ctx:
        def sb(name, shape, dt=F32):
            return ctx.enter_context(nc.sbuf_tensor(name, shape, dt))

        def pb(name):
            return ctx.enter_context(nc.psum_tensor(name, [P, 512], F32))

        def sem(name):
            return ctx.enter_context(nc.semaphore(name))

        wx1_s = sb("wx1_s", [P, KD, 5 * RLO])
        wx2_s = sb("wx2_s", [P, D])
        wx2g_s = sb("wx2g_s", [RLO, D])
        wr_s = sb("wr_s", [P, KD, NH * HK])
        ww1_s = sb("ww1_s", [P, KD, GLO])
        ww2_s = sb("ww2_s", [GLO, NH * HK])
        wk_s = sb("wk_s", [P, KD, NH * HK])
        wv_s = sb("wv_s", [P, KD, D])
        wg_s = sb("wg_s", [P, KD, D])
        wo_s = sb("wo_s", [P, VT, D])
        wf_s = sb("wf_s", [P, KD, D])
        bt_s = sb("bt_s", [RANK, D])
        bias_s = sb("bias_s", [P, D])
        vec_s = sb("vec_s", [P, 16])
        ident = sb("ident", [P, P])
        head_sel = sb("head_sel", [P, HH, VG, NH])
        head_mean = sb("head_mean", [P, VG, NH])
        eps_s = sb("eps_s", [P, 1])
        gn_half = sb("gn_half", [P, 2 * VT])
        alpha = sb("alpha", [P, KD])
        pool_cell = sb("pool_cell", [1, 32])
        dve_cell = sb("dve_cell", [1, 32])
        idx_i = sb("idx_i", [P, 4, TC], I32)
        idx_f = sb("idx_f", [P, 2, TC])
        idx_u = sb("idx_u", [P, 4, TC], U32)
        h = sb("h", [P, 4, TC, D])
        ag = sb("ag", [P, 4, TC, RANK])
        agT = sb("agT_s", [RANK, TC, P])
        stats = sb("stats", [P, 2, TC, 6])
        mv = sb("mv", [P, 2, TC, 2])
        sd = sb("sd", [P, 2, TC])
        rs = sb("rs", [P, 2, TC])
        xn = sb("xn", [P, TC, D])
        yn = xn
        xT = sb("xT", [P, 2, KD, TB + 1])
        delta = sb("delta", [P, KD, TB])
        mx = sb("mx", [P, MXRING, KD, TB])
        z0 = sb("z0", [P, TB])
        z1 = sb("z1", [RLO, TB])
        t2 = sb("t2", [GLO, TB])
        ew = sb("ew", [P, HH, TB])
        kT = sb("kT", [P, 2, HH, TB])
        vT = sb("vT", [P, 2, VT, TB])
        gate = sb("gate", [P, 2, VT, TB])
        ruk = sb("ruk", [P, HH, TB])
        bsb = sb("bsb", [P, TB])
        bv = sb("bv", [P, VT, TB])
        vB = sb("vB", [P, VRING, HH, TB])
        kv = sb("kv", [P, KVRING, HH, TB])
        state_flat = sb("state", [P, HV * HH * (TB + 1)])
        state = state_flat[:, :].rearrange("p (v a t) -> p v a t", v=HV, a=HH)
        wf = state_flat[:, 0:KD * D].rearrange("p (k n) -> p k n", k=KD)
        bw = state_flat[:, KD * D:2 * KD * D].rearrange("p (k n) -> p k n", k=KD)
        ob = sb("ob", [P, 2, VT, TB])
        sdo = sb("sdo", [P, TB])
        rg = sb("rg", [P, TB])
        yT = sb("yT", [P, VT, TB])
        y2T = sb("y2T", [P, KD, TC, P])
        sq = y2T[:, :, :, :].rearrange("p f c t -> p f (c t)")

        W = [pb(f"W{i}") for i in range(NW)]
        R = pb("R")
        DK = pb("DK")
        O = [pb("O0"), pb("O1")]
        r_t = R[:, :].rearrange("p (a t) -> p a t", a=HH)
        d_t = DK[:, :].rearrange("p (a t) -> p a t", a=HH)

        w_in = sem("weights_loaded")
        c_k = sem("constants_ready")
        c_cell = [sem("pool_cell_set"), sem("dve_cell_set")]
        c_sel = sem("selection_steps")
        c_f = sem("ffn_weight_steps")
        c_ft = sem("ffn_weight_turned")
        c_fc = sem("ffn_weight_copied")
        full = [sem(f"bank{i}_full") for i in range(NW)]
        free = [sem(f"bank{i}_emptied") for i in range(NW)]
        idx_in = [sem(f"idx_in{i}") for i in range(4)]
        idx_st = sem("idx_steps")
        rows_in = [sem(f"rows_in{i}") for i in range(4)]
        stored = [sem(f"stored{i}") for i in range(4)]
        v_h = sem("h_summed")
        v_st = sem("stats_done")
        v_mv = sem("mean_var_done")
        a_sd = sem("std_done")
        v_rs = sem("rstd_done")
        v_xn = sem("x_normed")
        p_col = sem("shift_column_set")
        p_delta = sem("delta_done")
        v_mx0 = sem("mix0_done")
        p_add = sem("mixed")
        a_th = sem("gate_tanh_done")
        a_d = sem("decay_set")
        pe_r = sem("r_ready")
        v_ruk = sem("ruk_done")
        p_bv = sem("bonus_done")
        vb_in = [sem(f"v_spread{i}") for i in range(VRING)]
        p_kv = sem("kv_done")
        v_c = sem("state_column_set")
        v_scan = sem("scanned")
        v_p = sem("products_done")
        pe_red = sem("heads_reduced")
        v_ob = sem("o_summed")
        a_sq = sem("o_squared")
        v_rg = sem("o_rstd_done")
        v_on = sem("o_normed")
        a_y = sem("o_scaled")
        p_y = sem("o_gated")
        v_h2 = sem("h_attn_summed")
        v_st2 = sem("stats2_done")
        v_mv2 = sem("mean_var2_done")
        a_sd2 = sem("std2_done")
        v_rs2 = sem("rstd2_done")
        v_yn = sem("y_normed")
        p_hb = sem("bias_added")

        NWEIGHTS = 14
        block = ctx.enter_context(nc.Block())

        def emptied(eng, b, name):
            wait(eng, free[BANK[name]], b.fill(name))

        def filled(eng, b, name):
            wait(eng, full[BANK[name]], b.fill(name))
            return W[BANK[name]]

        def take_wait(ops, cells, taken):
            taken.append(len(taken) + 1)
            ops.tensor_tensor(cells[:, taken[-1]:taken[-1] + 1], cells[:, 0:1], cells[:, 0:1], ALU.add)

        @block.sync
        def _(sp):
            for dst, src in ((vec_s[:, :], vecs), (bt_s[:, :], b_tok), (wx1_s[:, :, :], wx1.rearrange("(k p) n -> p k n", p=P)),
                             (wx2_s[:, :], wx2[0:P, :]), (wx2g_s[:, :], wx2[P:P + RLO, :]),
                             (ww1_s[:, :, :], ww1.rearrange("(k p) n -> p k n", p=P)), (ww2_s[:, :], ww2),
                             (wk_s[:, :, :], wk.rearrange("(k p) n -> p k n", p=P)),
                             (wv_s[:, :, :], wv.rearrange("(k p) n -> p k n", p=P)),
                             (wg_s[:, :, :], wg.rearrange("(k p) n -> p k n", p=P)),
                             (wr_s[:, :, :], wr.rearrange("(k p) n -> p k n", p=P)),
                             (wo_s[:, :, :], wo.rearrange("(k p) n -> p k n", p=P)),
                             (wf, w_ffn.rearrange("(k p) n -> p k n", p=P)),
                             (bias_s[:, :], b_ffn.to_broadcast([P, D]))):
                sp.dma_start(dst, src).then_inc(w_in, 16)

            def load_idx(b, _):
                q = b.off % 4
                src = x[bass.ds(sp.snap(b.times(1)), 1), :, :].rearrange("b p c -> (b p) c") if b.turn is not None else x[b.off, :, :]
                wait(sp, idx_st, b.times(3, 3 - 12))
                sp.dma_start(idx_i[:, q, :], src).then_inc(idx_in[q], 16)

            def spread(b, v):
                if v == 0:
                    emptied(sp, b, "pv1")
                else:
                    wait(sp, p_kv, b.times(HV, v + 2 - VRING))
                for hh in range(HH):
                    r0 = NH * (v % VG) + NH // HH * hh
                    sp.dma_start(vB[:, v % VRING, hh, :],
                                 vT[r0:r0 + NH // HH, b.off % 2, v // VG:v // VG + 1, :].to_broadcast([NH // HH, HK, TB]))\
                        .then_inc(vb_in[v % VRING], 16)

            whole_run(sp, {"sp_idx": load_idx, "sp_spread": spread})

        @block.gpsimd
        def _(pool):
            pool_taken = []
            nc.gpsimd.memset(pool_cell[:, :], 0.0).then_inc(c_cell[0], 1)
            pool.wait_ge(c_cell[0], 1)
            nc.gpsimd.memset(ident[:, :], 0.0).then_inc(c_sel, 1)
            nc.gpsimd.memset(head_sel[:, :, :, :], 1.0).then_inc(c_sel, 1)
            nc.gpsimd.memset(head_mean[:, :, :], 0.0).then_inc(c_sel, 1)
            nc.gpsimd.memset(eps_s[:, :], EPS).then_inc(c_sel, 1)
            pool.wait_ge(c_sel, 4)
            count = 4
            nc.gpsimd.affine_select(out=ident[:, :], in_=ident[:, :], compare_op=ALU.not_equal, fill=1.0, base=0,
                                    pattern=[[-1, P]], channel_multiplier=1).then_inc(c_k, 1)
            for hh in range(HH):
                nc.gpsimd.affine_select(out=head_sel[:, hh, :, :], in_=head_sel[:, hh, :, :], compare_op=ALU.is_ge, fill=0.0,
                                        base=HK * NH // HH * hh, pattern=[[0, VG], [-HK, NH]], channel_multiplier=1).then_inc(c_sel, 1)
                count += 1
                pool.wait_ge(c_sel, count)
                nc.gpsimd.affine_select(out=head_sel[:, hh, :, :], in_=head_sel[:, hh, :, :], compare_op=ALU.is_ge, fill=0.0,
                                        base=HK - 1 - HK * NH // HH * hh, pattern=[[0, VG], [HK, NH]], channel_multiplier=-1).then_inc(c_k, 1)
            for vi in range(VG):
                ins = nc.gpsimd.affine_select(out=head_mean[:, :, :], in_=head_mean[:, :, :], compare_op=ALU.not_equal, fill=1.0 / HV,
                                              base=-NH * vi, pattern=[[0, VG], [-1, NH]], channel_multiplier=1)
                if vi < VG - 1:
                    ins.then_inc(c_sel, 1)
                    count += 1
                    pool.wait_ge(c_sel, count)
                else:
                    ins.then_inc(c_k, 1)

            def gather(b, _):
                q = b.off % 4
                wait(pool, stored[q], b.round(4, 16))
                wait(pool, idx_st, b.times(3, 3))
                take_wait(nc.gpsimd, pool_cell, pool_taken)
                for c in range(TC):
                    nc.gpsimd.indirect_dma_start(h[:, q, c, :], None, w_tok, bass.IndirectOffsetOnAxis(ap=idx_u[:, q, c:c + 1], axis=0))\
                        .then_inc(rows_in[q], 16)
                    nc.gpsimd.indirect_dma_start(ag[:, q, c, :], None, a_tok, bass.IndirectOffsetOnAxis(ap=idx_u[:, q, c:c + 1], axis=0))\
                        .then_inc(rows_in[q], 16)

            def shift_difference(n, _):
                q = n.off % 2
                emptied(pool, n, "xT1")
                take_wait(nc.gpsimd, pool_cell, pool_taken)
                if n.off % PER_SEQ == 0:
                    nc.gpsimd.memset(xT[:, q, :, 0:1], 0.0).then_inc(p_col, 1)
                else:
                    nc.gpsimd.tensor_copy(xT[:, q, :, 0:1], xT[:, 1 - q, :, TB:TB + 1]).then_inc(p_col, 1)
                if n.off > 0:
                    emptied(pool, n + -1, "mu4b")
                pool.wait_ge(p_col, n.times(1, 1))
                nc.gpsimd.tensor_tensor(delta[:, :, :], xT[:, q, :, 0:TB], xT[:, q, :, 1:TB + 1], ALU.subtract).then_inc(p_delta, 1)

            def mix_add(n, a):
                emptied(pool, n, f"mu{a}b")
                m = mx[:, (1 + a) % MXRING, :, :]
                nc.gpsimd.tensor_tensor(m, m, xT[:, n.off % 2, :, 1:TB + 1], ALU.add).then_inc(p_add, 1)

            def key_value(j, v):
                if v == 0:
                    emptied(pool, j, "pk")
                if v % 2 == 0:
                    wait(pool, v_scan, j.times(HV, v + 2 - KVRING))
                wait(pool, vb_in[v % VRING], j.times(32 * HV // VRING, 32 * (v // VRING + 1)))
                nc.gpsimd.tensor_tensor(kv[:, v % KVRING, :, :], vB[:, v % VRING, :, :], kT[:, j.off % 2, :, :], ALU.mult)\
                    .then_inc(p_kv, 1)

            def bonus(j, _):
                emptied(pool, j, "pv1")
                wait(pool, v_ob, j.times(2))
                emptied(pool, j, "bs")
                nc.gpsimd.tensor_tensor(bv[:, :, :], vT[:, j.off % 2, :, :],
                                        bsb[:, :].rearrange("p (m t) -> p m t", m=1).to_broadcast([P, VT, TB]), ALU.mult)\
                    .then_inc(p_bv, 1)

            def gated(t, _):
                wait(pool, a_y, t.times(1, 1))
                nc.gpsimd.tensor_tensor(yT[:, :, :], yT[:, :, :], gate[:, t.off % 2, :, :], ALU.mult).then_inc(p_y, 1)

            def add_bias(t, _):
                wait(pool, v_yn, t.times(1, 1))
                q = t.off % 4
                nc.gpsimd.tensor_tensor(h[:, q, :, :], h[:, q, :, :],
                                        bias_s[:, :].rearrange("p (c d) -> p c d", c=1).to_broadcast([P, TC, D]), ALU.add)\
                    .then_inc(p_hb, 1)

            whole_run(pool, {"gp_gather": gather, "gp_delta": shift_difference, "gp_add": mix_add, "gp_kv": key_value,
                             "gp_bonus": bonus, "gp_gate": gated, "gp_bias": add_bias})

        @block.scalar
        def _(act):
            act.wait_ge(w_in, 16 * NWEIGHTS)
            act.wait_ge(c_sel, 4)
            nc.scalar.mul(gn_half[:, :], vec_s[:, NC_GW:NC_GW + 2 * VT], 0.5).then_inc(c_k, 1)

            def take(b, name, dst, src, func=ACT.Copy, last=True, **more):
                w = filled(act, b, name)
                ins = nc.scalar.activation(dst, src(w), func, **more)
                if last:
                    ins.then_inc(free[BANK[name]], 1)

            def lora_rows(n, _):
                take(n, "agT", agT[:, :, :], lambda w: w[0:RANK, 0:TB].rearrange("p (c t) -> p c t", c=TC))

            def deviation1(n, _):
                wait(act, v_mv, n.times(1, 1))
                nc.scalar.activation(sd[:, 0, :], mv[:, 0, :, 1], ACT.Sqrt, bias=eps_s[:, 0:1]).then_inc(a_sd, 1)

            def deviation2(t, _):
                wait(act, v_mv2, t.times(1, 1))
                nc.scalar.activation(sd[:, 1, :], mv[:, 1, :, 1], ACT.Sqrt, bias=eps_s[:, 0:1]).then_inc(a_sd2, 1)

            def x_turned(n, i):
                if i == 0:
                    wait(act, p_add, n.times(5, -5))
                    wait(act, p_col, n.times(1))
                take(n, f"xT{i}", xT[:, n.off % 2, 2 * i:2 * i + 2, 1:TB + 1].rearrange("p f (t c) -> p f t c", c=TC),
                     lambda w: w[:, :].rearrange("p (f c t) -> p f t c", f=2, c=TC))

            def z_tanh(n, _):
                take(n, "z", z0[:, :], lambda w: w[:, 0:TB], ACT.Tanh, last=False)
                take(n, "z", z1[:, :], lambda w: w[0:RLO, TB:2 * TB], ACT.Tanh)

            def decay_tanh(n, _):
                take(n, "pw", t2[:, :], lambda w: w[0:GLO, 0:TB], ACT.Tanh)

            def decay_exp(n, _):
                w = filled(act, n, "w2")
                for hh in range(HH):
                    ins = nc.scalar.activation(ew[:, hh, :], w[:, hh * TB:hh * TB + TB], ACT.Exp,
                                               bias=vec_s[:, NC_BW + hh:NC_BW + hh + 1])
                ins.then_inc(free[BANK["w2"]], 1)

            def decay(n, _):
                emptied(act, n, "w2")
                wait(act, v_scan, n.times(HV))
                nc.scalar.activation(DK[:, :], ew[:, :, :].rearrange("p a t -> p (a t)"), ACT.Exp, scale=-1.0).then_inc(a_d, 1)

            def k_out(n, _):
                wait(act, p_kv, n.times(HV, -HV))
                wait(act, v_ruk, n.times(1, -1))
                take(n, "pk", kT[:, n.off % 2, :, :], lambda w: w[:, :].rearrange("p (a t) -> p a t", a=HH))

            def v_out(n, i):
                if i == 0:
                    wait(act, p_kv, n.times(HV, -HV))
                    wait(act, p_bv, n.times(1, -1))
                take(n, f"pv{i}", vT[:, n.off % 2, 2 * i:2 * i + 2, :], lambda w: w[:, :].rearrange("p (m t) -> p m t", m=2))

            def gate_tanh(n, i):
                if i == 0:
                    wait(act, p_y, n.times(1, -1))
                w = filled(act, n, f"pg{i}")
                nc.scalar.activation(gate[:, n.off % 2, 2 * i:2 * i + 2, :], w[:, :].rearrange("p (m t) -> p m t", m=2),
                                     ACT.Tanh, scale=0.5).then_inc(a_th, 1)

            def bonus_sums(j, _):
                wait(act, p_bv, j.times(1))
                take(j, "bs", bsb[:, :], lambda w: w[:, 0:TB])

            def squares(t, _):
                emptied(act, t, "mean")
                if t.off > 0:
                    filled(act, t + -1, "f1")
                nc.scalar.activation(sq, ob[:, t.off % 2, :, :], ACT.Square).then_inc(a_sq, 1)

            def deviation_o(t, _):
                wait(act, v_rg, t.times(1))
                take(t, "var", sdo[:, :], lambda w: w[:, 0:TB], ACT.Sqrt, bias=eps_s[:, 0:1])

            def scaled(t, _):
                wait(act, v_on, t.times(1, 1))
                if t.off > 0:
                    filled(act, t + -1, "wo1")
                for m in range(VT):
                    ins = nc.scalar.activation(yT[:, m, :], ob[:, t.off % 2, m, :], ACT.Identity,
                                               bias=gn_half[:, VT + m:VT + m + 1], scale=gn_half[:, m:m + 1])
                ins.then_inc(a_y, 1)

            def y_turned(t, i):
                take(t, f"yT{i}", y2T[:, 2 * i:2 * i + 2, :, :], lambda w: w[:, :].rearrange("p (f c t) -> p f c t", f=2, c=TC))

            def store(t, _):
                at = bass.ds(t.times(1), 1) if t.turn is not None else slice(t.off, t.off + 1)
                emptied(act, t, "f1")
                act.dma_start(out[at, :, :].rearrange("b p n -> (b p) n"), h[:, t.off % 4, :, :].rearrange("p c d -> p (c d)"))\
                    .then_inc(stored[t.off % 4], 16)

            whole_run(act, {"act_agT": lora_rows, "act_sd1": deviation1, "act_sd2": deviation2, "act_xT": x_turned, "act_z": z_tanh,
                            "act_t2": decay_tanh, "act_ew": decay_exp, "act_d": decay, "act_k": k_out, "act_v": v_out,
                            "act_th": gate_tanh, "act_bs": bonus_sums, "act_sq": squares, "act_sdo": deviation_o,
                            "act_y": scaled, "act_yT": y_turned, "act_store": store})
            for q in range(4):
                act.wait_ge(stored[q], 16 * (NBLK // 4))

        @block.vector
        def _(dve):
            dve_taken = []
            nc.vector.memset(dve_cell[:, :], 0.0).then_inc(c_cell[1], 1)
            dve.wait_ge(c_cell[1], 1)
            dve.wait_ge(w_in, 16 * NWEIGHTS)
            nc.vector.tensor_reduce(alpha[:, :], wf, AX.X, ALU.add, apply_absolute_value=True).then_inc(c_f, 1)
            dve.wait_ge(c_f, 1)
            nc.vector.tensor_scalar(alpha[:, :], alpha[:, :], 1.0 / D, None, ALU.mult).then_inc(c_f, 1)
            nc.vector.tensor_scalar(bw, wf, 0.0, 2.0, ALU.is_ge, ALU.mult).then_inc(c_f, 1)
            dve.wait_ge(c_f, 3)
            for f in range(KD):
                nc.vector.tensor_scalar(bw[:, f, :], bw[:, f, :], -1.0, alpha[:, f:f + 1], ALU.add, ALU.mult).then_inc(c_f, 1)
            dve.wait_ge(c_f, 3 + KD)
            nc.vector.tensor_tensor(bw, bw, wf, ALU.subtract).then_inc(c_f, 1)
            dve.wait_ge(c_f, 4 + KD)
            nc.vector.tensor_tensor(bw, bw, wf, ALU.add).then_inc(c_f, 1)
            for f in range(KD):
                dve.wait_ge(c_ft, f + 1)
                nc.vector.tensor_copy(wf_s[:, f, :], W[f][:, :]).then_inc(c_fc, 1)

            def layer_stats(b, k, stats_sem, mv_sem, done):
                q = b.off % 4
                wait(dve, done, b.times(1))
                for c in range(TC):
                    ins = nc.vector.bn_stats(stats[:, k, c, :], h[:, q, c, :])
                ins.then_inc(stats_sem, 1)
                dve.wait_ge(stats_sem, b.times(1, 1))
                take_wait(nc.vector, dve_cell, dve_taken)
                for c in range(TC):
                    ins = nc.vector.bn_aggr(mv[:, k, c, :], stats[:, k, c, :])
                ins.then_inc(mv_sem, 1)

            def layer_norm(b, k, sd_sem, rs_sem, done):
                q = b.off % 4
                dve.wait_ge(sd_sem, b.times(1, 1))
                nc.vector.reciprocal(rs[:, k, :], sd[:, k, :]).then_inc(rs_sem, 1)
                dve.wait_ge(rs_sem, b.times(1, 1))
                for c in range(TC):
                    ins = nc.vector.tensor_scalar(xn[:, c, :], h[:, q, c, :], mv[:, k, c, 0:1], rs[:, k, c:c + 1],
                                                  ALU.subtract, ALU.mult)
                ins.then_inc(done, 1)

            def clamp_idx(b, _):
                q = b.off % 4
                wait(dve, idx_in[q], b.round(4, 16, 16))
                wait(dve, idx_st, b.times(3))
                wait(dve, rows_in[q], b.round(4, 64))
                nc.vector.tensor_scalar(idx_f[:, 0, :], idx_i[:, q, :], float(VOCAB - 1), float(-VOCAB), ALU.min, ALU.max).then_inc(idx_st, 1)
                dve.wait_ge(idx_st, b.times(3, 1))
                nc.vector.tensor_scalar(idx_f[:, 1, :], idx_f[:, 0, :], 0.0, float(VOCAB), ALU.is_lt, ALU.mult).then_inc(idx_st, 1)
                dve.wait_ge(idx_st, b.times(3, 2))
                nc.vector.tensor_tensor(idx_u[:, q, :], idx_f[:, 0, :], idx_f[:, 1, :], ALU.add).then_inc(idx_st, 1)

            def add_fill(b, name, c):
                w = filled(dve, b, name)
                hc = h[:, b.off % 4, c, :]
                nc.vector.tensor_tensor(hc, hc, w[:, :], ALU.add).then_inc(free[BANK[name]], 1)

            def add_lora(n, c):
                add_fill(n, f"lora{c}", c)

            def add_attention(t, c):
                add_fill(t, f"wo{c}", c)

            def add_ffn(t, c):
                if c == 0:
                    dve.wait_ge(p_hb, t.times(1, 1))
                add_fill(t, f"f{c}", c)

            def stats1(n, _):
                emptied(dve, n, "lora1")
                layer_stats(n, 0, v_st, v_mv, v_xn)

            def stats2(t, _):
                emptied(dve, t, "wo1")
                layer_stats(t, 1, v_st2, v_mv2, v_yn)

            def norm1(n, _):
                if n.off + Y_TURNED_BEFORE >= 0:
                    filled(dve, n + Y_TURNED_BEFORE, "yT1")
                layer_norm(n, 0, a_sd, v_rs, v_xn)

            def norm2(t, _):
                if t.off + X_TURNED_BEFORE < NBLK:
                    filled(dve, t + X_TURNED_BEFORE, "xT1")
                layer_norm(t, 1, a_sd2, v_rs2, v_yn)

            def mix0(n, _):
                if n.off > 0:
                    filled(dve, n + -1, "pv1")
                dve.wait_ge(p_delta, n.times(1, 1))
                for f in range(KD):
                    ins = nc.vector.scalar_tensor_tensor(mx[:, 0, f, :], delta[:, f, :], vec_s[:, NC_MU + f:NC_MU + f + 1],
                                                         xT[:, n.off % 2, f, 1:TB + 1], ALU.mult, ALU.add)
                ins.then_inc(v_mx0, 1)

            def mix_times_delta(n, a):
                if a == 0 and n.off > 0:
                    filled(dve, n + -1, "pg1")
                if a == 1:
                    wait(dve, pe_r, n.times(1))
                if a >= 2:
                    filled(dve, n, ("z", "pw", "pk")[a - 2])
                for i, name in enumerate((f"mu{a}a", f"mu{a}b")):
                    w = filled(dve, n, name)
                    nc.vector.tensor_tensor(mx[:, (1 + a) % MXRING, 2 * i:2 * i + 2, :], w[:, :].rearrange("p (f t) -> p f t", f=2),
                                            delta[:, 2 * i:2 * i + 2, :], ALU.mult).then_inc(free[BANK[name]], 1)

            def gate_mult(n, i):
                dve.wait_ge(a_th, n.times(2, i + 1))
                gt = gate[:, n.off % 2, 2 * i:2 * i + 2, :]
                nc.vector.scalar_tensor_tensor(gt, gt, 1.0, W[BANK[f"pg{i}"]][:, :].rearrange("p (m t) -> p m t", m=2), ALU.add, ALU.mult)\
                    .then_inc(free[BANK[f"pg{i}"]], 1)

            def scan(j, v):
                if v % VG == 0:
                    wait(dve, pe_red, j.times(VT, v // VG + 1 - VT))
                    if j.off % PER_SEQ == 0:
                        nc.vector.memset(state[:, v:v + VG, :, 0:1], 0.0).then_inc(v_c, 1)
                    else:
                        nc.vector.tensor_copy(state[:, v:v + VG, :, 0:1], state[:, v:v + VG, :, TB:TB + 1]).then_inc(v_c, 1)
                    dve.wait_ge(v_c, j.times(VT, v // VG + 1))
                if v == 0:
                    dve.wait_ge(a_d, j.times(1, 1))
                dve.wait_ge(p_kv, j.times(HV, v + 1))
                for hh in range(HH):
                    ins = nc.vector.tensor_tensor_scan(state[:, v, hh, 1:TB + 1], d_t[:, hh, :], kv[:, v % KVRING, hh, :],
                                                       state[:, v, hh, 0:1], ALU.mult, ALU.add)
                ins.then_inc(v_scan, 1)

            def products(j, v):
                dve.wait_ge(v_scan, j.times(HV, v + 1))
                if v == 0:
                    dve.wait_ge(pe_r, j.times(1, 1))
                nc.vector.tensor_tensor(state[:, v, :, 0:TB], state[:, v, :, 0:TB], r_t, ALU.mult).then_inc(v_p, 1)

            def bonus_product(j, _):
                emptied(dve, j, "pk")
                dve.wait_ge(pe_r, j.times(1, 1))
                for hh in range(HH):
                    ins = nc.vector.scalar_tensor_tensor(ruk[:, hh, :], r_t[:, hh, :], vec_s[:, NC_U + hh:NC_U + hh + 1],
                                                         kT[:, j.off % 2, hh, :], ALU.mult, ALU.mult)
                ins.then_inc(v_ruk, 1)

            def sum_o(j, i):
                wait(dve, a_y, j.times(1, -1))
                dve.wait_ge(p_bv, j.times(1, 1))
                dve.wait_ge(pe_red, j.times(VT, 2 * i + 2))
                nc.vector.tensor_tensor(ob[:, j.off % 2, 2 * i:2 * i + 2, :], bv[:, 2 * i:2 * i + 2, :],
                                        O[i][:, :].rearrange("p (m t) -> p m t", m=2), ALU.add).then_inc(v_ob, 1)

            def centre(t, _):
                w = filled(dve, t, "mean")
                o = ob[:, t.off % 2, :, :]
                nc.vector.tensor_tensor(o, o, w[:, 0:TB].rearrange("p (m t) -> p m t", m=1).to_broadcast([P, VT, TB]),
                                        ALU.subtract).then_inc(free[BANK["mean"]], 1)

            def normalise(t, _):
                wait(dve, v_on, t.times(1))
                emptied(dve, t, "var")
                nc.vector.reciprocal(rg[:, :], sdo[:, :]).then_inc(v_rg, 1)
                dve.wait_ge(v_rg, t.times(1, 1))
                o = ob[:, t.off % 2, :, :]
                nc.vector.tensor_tensor(o, o, rg[:, :].rearrange("p (m t) -> p m t", m=1).to_broadcast([P, VT, TB]), ALU.mult)\
                    .then_inc(v_on, 1)

            whole_run(dve, {"dv_idx": clamp_idx, "dv_lora": add_lora, "dv_st1": stats1, "dv_n1": norm1, "dv_mix0": mix0,
                            "dv_mus": mix_times_delta, "dv_gate": gate_mult, "dv_scan": scan, "dv_prod": products,
                            "dv_ruk": bonus_product, "dv_ob": sum_o, "dv_oc": centre, "dv_on": normalise,
                            "dv_h2": add_attention, "dv_st2": stats2, "dv_n2": norm2, "dv_out": add_ffn})

        @block.tensor
        def _(pe):
            pe.wait_ge(w_in, 16 * NWEIGHTS)
            pe.wait_ge(c_k, 5)
            pe.wait_ge(c_f, 5 + KD)
            for f in range(KD):
                for o in range(KD):
                    ins = nc.tensor.transpose(W[f][:, o * P:o * P + P],
                                              bw[:, o, f * P:f * P + P], ident[:, :])
                ins.then_inc(c_ft, 1)
            pe.wait_ge(c_fc, KD)

            def fill(b, name):
                wait(pe, free[BANK[name]], b.fill(name, -1))
                return W[BANK[name]], full[BANK[name]]

            def project(w, bank, src, m, cols=P):
                for k in range(KD):
                    ins = nc.tensor.matmul(bank, w[:, k, m * P:m * P + cols], src[:, k, :], start=(k == 0), stop=(k == KD - 1))
                return ins

            def turn(w, src, i):
                for g in range(2):
                    for c in range(TC):
                        ins = nc.tensor.transpose(w[:, (2 * g + c) * P:(2 * g + c + 1) * P],
                                                  src[:, c, (2 * i + g) * P:(2 * i + g + 1) * P], ident[:, :])
                return ins

            def lora_turn(n, _):
                q = n.off % 4
                wait(pe, rows_in[q], n.round(4, 64, 64))
                w, f = fill(n, "agT")
                for c in range(TC):
                    ins = nc.tensor.transpose(w[0:RANK, c * P:c * P + P], ag[:, q, c, :], ident[:, :])
                ins.then_inc(f, 1)

            def lora(n, c):
                emptied(pe, n, "agT")
                w, f = fill(n, f"lora{c}")
                nc.tensor.matmul(w[:, :], agT[:, c, :], bt_s[:, :], start=True, stop=True).then_inc(f, 1)

            def turn_x(n, i):
                pe.wait_ge(v_xn, n.times(1, 1))
                w, f = fill(n, f"xT{i}")
                turn(w, xn, i).then_inc(f, 1)

            def turn_y(t, i):
                pe.wait_ge(v_yn, t.times(1, 1))
                w, f = fill(t, f"yT{i}")
                turn(w, xn, i).then_inc(f, 1)

            def token_shift_rank(n, _):
                pe.wait_ge(v_mx0, n.times(1, 1))
                w, f = fill(n, "z")
                project(wx1_s, w[:, 0:TB], mx[:, 0, :, :], 0)
                project(wx1_s, w[0:RLO, TB:2 * TB], mx[:, 0, :, :], 1, RLO).then_inc(f, 1)

            def mus(n, a):
                emptied(pe, n, "z")
                both = [a, a + 1] if a + 1 < len(MIXES) else [a]
                for i in range(2):
                    banks = [fill(n, f"mu{c}{'ab'[i]}") for c in both]
                    for g in range(2):
                        f0 = (2 * i + g) * P
                        for c, (w, f) in zip(both, banks):
                            m = MIXES[c]
                            r0 = RLO * m
                            w2, zz = (wx2g_s, z1[:, :]) if m == MIX_G else (wx2_s[r0:r0 + RLO, :], z0[r0:r0 + RLO, :])
                            ins = nc.tensor.matmul(w[:, g * TB:g * TB + TB], w2[:, f0:f0 + P], zz, start=True, stop=True)
                            if g == 1:
                                ins.then_inc(f, 1)

            def mixed(n, a):
                pe.wait_ge(p_add, n.times(5, a + 1))
                return mx[:, (1 + a) % MXRING, :, :]

            def proj(n, a):
                src = mixed(n, a)
                if MIXES[a] == MIX_W:
                    w, f = fill(n, "pw")
                    project(ww1_s, w[0:GLO, 0:TB], src, 0, GLO).then_inc(f, 1)
                if MIXES[a] == MIX_K:
                    w, f = fill(n, "pk")
                    for hh in range(HH):
                        ins = project(wk_s, w[:, hh * TB:hh * TB + TB], src, hh)
                    ins.then_inc(f, 1)
                if MIXES[a] == MIX_R:
                    wait(pe, v_p, n.times(HV))
                    for hh in range(HH):
                        ins = project(wr_s, R[:, hh * TB:hh * TB + TB], src, hh)
                    ins.then_inc(pe_r, 1)

            def proj_v(n, i):
                src = mixed(n, MIXES.index(MIX_V))
                w, f = fill(n, f"pv{i}")
                for g in range(2):
                    ins = project(wv_s, w[:, g * TB:g * TB + TB], src, 2 * i + g)
                ins.then_inc(f, 1)

            def proj_g(n, i):
                src = mixed(n, MIXES.index(MIX_G))
                w, f = fill(n, f"pg{i}")
                for g in range(2):
                    ins = project(wg_s, w[:, g * TB:g * TB + TB], src, 2 * i + g)
                ins.then_inc(f, 1)

            def decay_rank(n, _):
                emptied(pe, n, "pw")
                w, f = fill(n, "w2")
                for hh in range(HH):
                    ins = nc.tensor.matmul(w[:, hh * TB:hh * TB + TB], ww2_s[:, hh * P:hh * P + P], t2[:, :], start=True, stop=True)
                ins.then_inc(f, 1)

            def bonus_sum(j, _):
                pe.wait_ge(v_ruk, j.times(1, 1))
                w, f = fill(j, "bs")
                for hh in range(HH):
                    ins = nc.tensor.matmul(w[:, 0:TB], head_sel[:, hh, :, :].rearrange("p v h -> p (v h)"), ruk[:, hh, :],
                                           start=(hh == 0), stop=(hh == HH - 1))
                ins.then_inc(f, 1)

            def reduce_heads(j, m):
                if m % 2 == 0:
                    wait(pe, v_ob, j.times(2, m // 2 - 1))
                pe.wait_ge(v_p, j.times(HV, VG * (m + 1)))
                for hh in range(HH):
                    for vi in range(VG):
                        ins = nc.tensor.matmul(O[m // 2][NH * vi:NH * vi + NH, (m % 2) * TB:(m % 2) * TB + TB],
                                               head_sel[:, hh, 0, :], state[:, VG * m + vi, hh, 0:TB],
                                               start=(hh == 0), stop=(hh == HH - 1), tile_position=(0, NH * vi))
                ins.then_inc(pe_red, 1)

            def head_means(t, name, src):
                w, f = fill(t, name)
                for m in range(VT):
                    ins = nc.tensor.matmul(w[:, 0:TB], head_mean[:, :, :].rearrange("p v h -> p (v h)"), src[:, m, :],
                                           start=(m == 0), stop=(m == VT - 1))
                ins.then_inc(f, 1)

            def mean(t, _):
                pe.wait_ge(v_ob, t.times(2, 2))
                head_means(t, "mean", ob[:, t.off % 2, :, :])

            def variance(t, _):
                pe.wait_ge(a_sq, t.times(1, 1))
                head_means(t, "var", sq)

            def proj_o(t, c):
                pe.wait_ge(p_y, t.times(1, 1))
                w, f = fill(t, f"wo{c}")
                for m in range(VT):
                    ins = nc.tensor.matmul(w[:, :], yT[:, m, c:TB:TC], wo_s[:, m, :], start=(m == 0), stop=(m == VT - 1))
                ins.then_inc(f, 1)

            def ffn(t, c):
                emptied(pe, t, "yT1")
                w, f = fill(t, f"f{c}")
                for k in range(KD):
                    ins = nc.tensor.matmul(w[:, :], y2T[:, k, c, :], wf_s[:, k, :], start=(k == 0), stop=(k == KD - 1))
                ins.then_inc(f, 1)

            whole_run(pe, {"pe_agT": lora_turn, "pe_lora": lora, "pe_xT": turn_x, "pe_yT": turn_y, "pe_z": token_shift_rank,
                           "pe_mus": mus, "pe_proj": proj, "pe_pv": proj_v, "pe_pg": proj_g, "pe_w2": decay_rank,
                           "pe_bs": bonus_sum, "pe_red": reduce_heads, "pe_mean": mean, "pe_var": variance, "pe_wo": proj_o,
                           "pe_ffn": ffn})


_ORDER = ["x", "w_tok", "a_tok", "b_tok", "vecs", "wx1", "wx2", "wr", "ww1", "ww2", "wk", "wv", "wg", "wo", "w_ffn", "b_ffn"]


def kernel(x, L0_tok_W, L0_tok_A, L0_tok_B, L0_attn_mu_x, L0_attn_Wx1, L0_attn_Wx2, L0_attn_Wr, L0_attn_Ww1, L0_attn_Ww2,
           L0_attn_bw, L0_attn_Wk, L0_attn_Wv, L0_attn_Wg, L0_attn_bonus, L0_attn_gn_w, L0_attn_gn_b, L0_attn_Wo,
           L0_ffn_weight, L0_ffn_bias):
    import numpy as np
    from concourse import bacc
    from concourse.bass_utils import run_bass_kernel_spmd

    def columns(v):
        return np.asarray(v).reshape(-1, P).T

    def value_major(w):
        return np.asarray(w).reshape(-1, NH, HV).transpose(0, 2, 1).reshape(-1, D)

    gn = [columns(np.repeat(np.asarray(v), NH)) for v in (L0_attn_gn_w, L0_attn_gn_b)]
    given = {
        "x": np.asarray(x).reshape(NBLK, P, TC),
        "w_tok": L0_tok_W, "a_tok": L0_tok_A, "b_tok": L0_tok_B,
        "vecs": np.concatenate([columns(L0_attn_mu_x), columns(L0_attn_bonus), columns(L0_attn_bw)] + gn, axis=1),
        "wx1": L0_attn_Wx1, "wx2": np.asarray(L0_attn_Wx2).reshape(5 * RLO, D), "wr": L0_attn_Wr, "ww1": L0_attn_Ww1,
        "ww2": L0_attn_Ww2, "wk": L0_attn_Wk, "wv": value_major(L0_attn_Wv), "wg": value_major(L0_attn_Wg),
        "wo": value_major(np.asarray(L0_attn_Wo).T).T, "w_ffn": L0_ffn_weight, "b_ffn": np.asarray(L0_ffn_bias).reshape(1, D),
    }
    nc = bacc.Bacc("TRN2", target_bir_lowering=False, num_devices=1)
    arrays, args = {}, []
    for name in _ORDER:
        a = np.ascontiguousarray(given[name])
        arrays[f"in_{name}"] = a
        args.append(nc.dram_tensor(f"in_{name}", a.shape, mybir.dt.from_np(a.dtype), kind="ExternalInput").ap())
    args.append(nc.dram_tensor("out_h", (NBLK, P, TC * D), F32, kind="ExternalOutput").ap())
    tower_kernel(nc, *args)
    r = run_bass_kernel_spmd(nc, [arrays], core_ids=[0])
    return r.results[0]["out_h"].reshape(SEQS, SEQ, D)
```

```python
from contextlib import ExitStack

import concourse.bass as bass
from concourse import mybir

F32 = mybir.dt.float32
I32 = mybir.dt.int32
U32 = mybir.dt.uint32
ALU = mybir.AluOpType
ACT = mybir.ActivationFunctionType
AX = mybir.AxisListType

P = 128
SEQS, SEQ = 8, 1024
D = 512
KD = D // P
NH, HK, HV = 32, 8, 16
VG = 4
VT = HV // VG
HH = 2
RLO, GLO = 32, 64
RANK = 16
VOCAB = 32000
EPS = 1e-5
TB = 256
TC = TB // P
NBLK = SEQS * SEQ // TB
PER_SEQ = SEQ // TB
LOOPED = 4
VRING, KVRING, MXRING = 8, 4, 3
MIX_R, MIX_W, MIX_K, MIX_V, MIX_G = range(5)
MIXES = [MIX_W, MIX_K, MIX_V, MIX_G, MIX_R]
NC_MU, NC_U, NC_BW, NC_GW, NC_GB = 0, 4, 6, 8, 12
NW = 4

SCHEDULE = [
    ("act_ew", 0, -1), ("dv_lora", 1, 1), ("dv_st1", 0, 1), ("gp_kv", 1, -1), ("act_d", 0, -1), ("dv_scan", 0, -1),
    ("dv_ruk", 0, -1), ("sp_spread", 3, -1), ("dv_h2", 0, -2), ("pe_pg", 0, -1), ("dv_prod", 0, -1), ("dv_scan", 1, -1),
    ("dv_prod", 1, -1), ("gp_kv", 2, -1), ("sp_spread", 4, -1), ("pe_z", 0, 0), ("gp_kv", 3, -1), ("act_sd1", 0, 1),
    ("dv_scan", 2, -1), ("gp_kv", 4, -1), ("dv_h2", 1, -2), ("dv_st2", 0, -2), ("act_sd2", 0, -2), ("dv_scan", 3, -1),
    ("act_th", 0, -1), ("dv_prod", 2, -1), ("sp_spread", 5, -1), ("dv_prod", 3, -1), ("dv_n2", 0, -2), ("pe_yT", 0, -2),
    ("gp_kv", 5, -1), ("act_z", 0, 0), ("pe_bs", 0, -1), ("sp_spread", 6, -1), ("act_bs", 0, -1), ("sp_spread", 7, -1),
    ("gp_kv", 6, -1), ("dv_gate", 0, -1), ("gp_kv", 7, -1), ("dv_scan", 4, -1), ("dv_scan", 5, -1), ("sp_spread", 8, -1),
    ("pe_yT", 1, -2), ("gp_bias", 0, -2), ("sp_spread", 9, -1), ("act_yT", 0, -2), ("gp_kv", 8, -1), ("dv_prod", 4, -1),
    ("gp_kv", 9, -1), ("dv_scan", 6, -1), ("pe_pg", 1, -1), ("act_yT", 1, -2), ("sp_spread", 10, -1), ("dv_prod", 5, -1),
    ("dv_scan", 7, -1), ("act_th", 1, -1), ("pe_mus", 0, 0), ("dv_scan", 8, -1), ("dv_n1", 0, 1), ("dv_gate", 1, -1),
    ("sp_spread", 11, -1), ("pe_red", 0, -1), ("dv_prod", 6, -1), ("dv_mus", 4, 0), ("sp_spread", 12, -1), ("dv_mus", 2, 0),
    ("pe_ffn", 0, -2), ("dv_scan", 9, -1), ("dv_mus", 0, 0), ("gp_kv", 10, -1), ("sp_spread", 13, -1), ("pe_mus", 1, 0),
    ("dv_scan", 10, -1), ("dv_prod", 7, -1), ("gp_kv", 11, -1), ("dv_out", 0, -2), ("gp_bonus", 0, -1), ("dv_mus", 1, 0),
    ("dv_mus", 3, 0), ("pe_red", 1, -1), ("dv_prod", 8, -1), ("gp_kv", 12, -1), ("pe_xT", 0, 1), ("sp_spread", 14, -1),
    ("dv_mus", 5, 0), ("pe_xT", 1, 1), ("gp_kv", 13, -1), ("dv_scan", 11, -1), ("dv_prod", 9, -1), ("gp_add", 0, 0),
    ("act_xT", 0, 1), ("dv_prod", 10, -1), ("pe_ffn", 1, -2), ("dv_scan", 12, -1), ("pe_proj", 0, 0), ("dv_prod", 11, -1),
    ("pe_red", 2, -1), ("gp_add", 1, 0), ("dv_prod", 12, -1), ("act_xT", 1, 1), ("gp_kv", 14, -1), ("dv_out", 1, -2),
    ("dv_scan", 13, -1), ("sp_spread", 15, -1), ("dv_scan", 14, -1), ("gp_kv", 15, -1), ("pe_proj", 1, 0),
    ("dv_scan", 15, -1), ("act_t2", 0, 0), ("dv_prod", 13, -1), ("dv_prod", 14, -1), ("act_store", 0, -2), ("pe_mus", 2, 0),
    ("act_k", 0, 0), ("sp_idx", 0, 3), ("pe_mus", 3, 0), ("dv_idx", 0, 3), ("dv_prod", 15, -1), ("gp_add", 2, 0),
    ("dv_mus", 6, 0), ("pe_red", 3, -1), ("dv_ob", 0, -1), ("dv_ob", 1, -1), ("act_sq", 0, -1), ("dv_mus", 8, 0),
    ("pe_pv", 0, 0), ("dv_mus", 7, 0), ("pe_var", 0, -1), ("gp_gather", 0, 2), ("dv_mus", 9, 0), ("pe_agT", 0, 2),
    ("act_sdo", 0, -1), ("dv_on", 0, -1), ("pe_pv", 1, 0), ("act_agT", 0, 2), ("gp_add", 3, 0), ("act_v", 0, 0),
    ("gp_delta", 0, 1), ("pe_lora", 0, 2), ("act_y", 0, -1), ("act_v", 1, 0), ("sp_spread", 0, 0), ("sp_spread", 1, 0),
    ("gp_add", 4, 0), ("dv_mix0", 0, 1), ("pe_w2", 0, 0), ("pe_proj", 4, 0), ("gp_gate", 0, -1), ("dv_lora", 0, 2),
    ("gp_kv", 0, 0), ("pe_wo", 0, -1), ("pe_wo", 1, -1), ("sp_spread", 2, 0),
]
FILLS = {
    ("pe_agT", 0): ["agT"], ("pe_lora", 0): ["lora0", "lora1"],
    ("pe_xT", 0): ["xT0"], ("pe_xT", 1): ["xT1"], ("pe_z", 0): ["z"],
    ("pe_mus", 0): ["mu0a", "mu1a", "mu2a"], ("pe_mus", 1): ["mu0b", "mu1b", "mu2b"],
    ("pe_mus", 2): ["mu3a", "mu4a"], ("pe_mus", 3): ["mu3b", "mu4b"],
    ("pe_proj", 0): ["pw"], ("pe_proj", 1): ["pk"], ("pe_pv", 0): ["pv0"], ("pe_pv", 1): ["pv1"],
    ("pe_pg", 0): ["pg0"], ("pe_pg", 1): ["pg1"], ("pe_w2", 0): ["w2"], ("pe_bs", 0): ["bs"],
    ("pe_var", 0): ["var"], ("pe_wo", 0): ["wo0"], ("pe_wo", 1): ["wo1"],
    ("pe_yT", 0): ["yT0"], ("pe_yT", 1): ["yT1"], ("pe_ffn", 0): ["f0"], ("pe_ffn", 1): ["f1"],
}


MOST, LEAST = max(x[2] for x in SCHEDULE), min(x[2] for x in SCHEDULE)
FIRST_LOOPED = 1 - LEAST


def fill_places():
    bank, per = {}, [0] * NW
    order = [(n, stage) for what, a, stage in SCHEDULE for n in FILLS.get((what, a), [])]
    for i, (n, stage) in enumerate(order):
        bank[n] = i % NW
        per[i % NW] += 1
    count, seen = {n: {} for n, _ in order}, [0] * NW
    for s in range(-MOST, NBLK - LEAST):
        for n, stage in order:
            if 0 <= s + stage < NBLK:
                seen[bank[n]] += 1
                count[n][s + stage] = seen[bank[n]]
    return bank, count, per


BANK, COUNT, PER = fill_places()
POS = {x[:2]: (i, x[2]) for i, x in enumerate(SCHEDULE)}
Y_TURNED_BEFORE = POS["dv_n2", 0][1] - POS["dv_n1", 0][1] - (POS["dv_n2", 0][0] > POS["dv_n1", 0][0])
X_TURNED_BEFORE = POS["dv_n1", 0][1] - POS["dv_n2", 0][1] - (POS["dv_n1", 0][0] > POS["dv_n2", 0][0])


class Block:

    def __init__(self, off, turn=None):
        self.off, self.turn = off, turn

    def __add__(self, n):
        return Block(self.off + n, self.turn)

    def times(self, per, c=0):
        const = per * self.off + c
        if self.turn is None:
            return const
        assert const > 0
        return self.turn * (per * LOOPED) + const

    def round(self, n, per, c=0):
        const = per * (self.off // n) + c
        if self.turn is None:
            return const
        assert const > 0
        return self.turn * (per * (LOOPED // n)) + const

    def fill(self, name, c=0):
        const = COUNT[name][self.off] + c
        if self.turn is None:
            return const
        per = PER[BANK[name]] * LOOPED
        assert const > 0 and COUNT[name][self.off + LOOPED] + c - const == per
        return self.turn * per + const


def wait(eng, sem, value):
    if isinstance(value, int) and value <= 0:
        return
    eng.wait_ge(sem, value)


def whole_run(eng, pieces):
    def step(off, turn=None):
        for what, a, stage in SCHEDULE:
            b = off + stage
            if what in pieces and (turn is not None or 0 <= b < NBLK):
                pieces[what](Block(b, turn), a)

    turns = (NBLK - MOST - FIRST_LOOPED) // LOOPED
    for s in range(-MOST, FIRST_LOOPED):
        step(s)
    with eng.Fori(0, turns) as turn:
        for u in range(LOOPED):
            step(FIRST_LOOPED + u, turn)
    for s in range(FIRST_LOOPED + turns * LOOPED, NBLK - LEAST):
        step(s)


def tower_kernel(nc, x, w_tok, a_tok, b_tok, vecs, wx1, wx2, wr, ww1, ww2, wk, wv, wg, wo, w_ffn, b_ffn, out):
    ctx = ExitStack()
    with ctx:
        def sb(name, shape, dt=F32):
            return ctx.enter_context(nc.sbuf_tensor(name, shape, dt))

        def pb(name):
            return ctx.enter_context(nc.psum_tensor(name, [P, 512], F32))

        def sem(name):
            return ctx.enter_context(nc.semaphore(name))

        wx1_s = sb("wx1_s", [P, KD, 5 * RLO])
        wx2_s = sb("wx2_s", [P, D])
        wx2g_s = sb("wx2g_s", [2 * RLO, D])
        wr_s = sb("wr_s", [P, KD, NH * HK])
        ww1_s = sb("ww1_s", [P, KD, GLO])
        ww2_s = sb("ww2_s", [GLO, NH * HK])
        wk_s = sb("wk_s", [P, KD, NH * HK])
        wv_s = sb("wv_s", [P, KD, D])
        wg_s = sb("wg_s", [P, KD, D])
        wo_s = sb("wo_s", [P, VT, D])
        wf_s = sb("wf_s", [P, KD, D])
        bt_s = sb("bt_s", [P // TC + RANK, D])
        bias_s = sb("bias_s", [P, D])
        vec_s = sb("vec_s", [P, 16])
        ident = sb("ident", [P, P])
        head_sel = sb("head_sel", [P, HH, VG, NH])
        head_mean = sb("head_mean", [P, VG, NH])
        eps_s = sb("eps_s", [P, 1])
        gn_half = sb("gn_half", [P, 2 * VT])
        alpha = sb("alpha", [P, KD])
        pool_cell = sb("pool_cell", [1, 32])
        dve_cell = sb("dve_cell", [1, 32])
        idx_i = sb("idx_i", [P, 4, TC], I32)
        idx_f = sb("idx_f", [P, 2, TC])
        idx_u = sb("idx_u", [P, 4, TC], U32)
        h = sb("h", [P, 4, TC, D])
        ag = sb("ag", [P, 4, TC, P // TC])
        agT = sb("agT_s", [P, P])
        stats = sb("stats", [P, 2, TC, 6])
        mv = sb("mv", [P, 2, TC, 2])
        sd = sb("sd", [P, 2, TC])
        rs = sb("rs", [P, 2, TC])
        xn = sb("xn", [P, TC, D])
        yn = xn
        xT = sb("xT", [P, 2, KD, TB + 1])
        delta = sb("delta", [P, KD, TB])
        mx = sb("mx", [P, MXRING, KD, TB])
        z0 = sb("z0", [P, TB])
        z1 = sb("z1", [2 * RLO, TB])
        t2 = sb("t2", [GLO, TB])
        ew = sb("ew", [P, HH, TB])
        kT = sb("kT", [P, 2, HH, TB])
        vT = sb("vT", [P, 2, VT, TB])
        gate = sb("gate", [P, 2, VT, TB])
        ruk = sb("ruk", [P, HH, TB])
        bsb = sb("bsb", [P, TB])
        bv = sb("bv", [P, VT, TB])
        vB = sb("vB", [P, VRING, HH, TB])
        kv = sb("kv", [P, KVRING, HH, TB])
        state_flat = sb("state", [P, HV * HH * (TB + 1)])
        state = state_flat[:, :].rearrange("p (v a t) -> p v a t", v=HV, a=HH)
        wv_mean = state_flat[:, 2 * KD * D:2 * KD * D + KD * NH].rearrange("p (k h) -> p k h", k=KD)
        wf = state_flat[:, 0:KD * D].rearrange("p (k n) -> p k n", k=KD)
        bw = state_flat[:, KD * D:2 * KD * D].rearrange("p (k n) -> p k n", k=KD)
        ob = sb("ob", [P, 2, VT, TB])
        sdo = sb("sdo", [P, TB])
        rg = sb("rg", [P, TB])
        yT = sb("yT", [P, VT, TB])
        y2T = sb("y2T", [P, KD, TC, P])
        sq = y2T[:, :, :, :].rearrange("p f c t -> p f (c t)")

        W = [pb(f"W{i}") for i in range(NW)]
        R = pb("R")
        DK = pb("DK")
        O = [pb("O0"), pb("O1")]
        r_t = R[:, :].rearrange("p (a t) -> p a t", a=HH)
        d_t = DK[:, :].rearrange("p (a t) -> p a t", a=HH)

        w_in = sem("weights_loaded")
        c_k = sem("constants_ready")
        c_cell = [sem("pool_cell_set"), sem("dve_cell_set")]
        c_sel = sem("selection_steps")
        c_v = sem("value_weight_centred")
        c_f = sem("ffn_weight_steps")
        c_ft = sem("ffn_weight_turned")
        c_fc = sem("ffn_weight_copied")
        full = [sem(f"bank{i}_full") for i in range(NW)]
        free = [sem(f"bank{i}_emptied") for i in range(NW)]
        idx_in = [sem(f"idx_in{i}") for i in range(4)]
        idx_st = sem("idx_steps")
        rows_in = [sem(f"rows_in{i}") for i in range(4)]
        stored = [sem(f"stored{i}") for i in range(4)]
        v_h = sem("h_summed")
        v_st = sem("stats_done")
        v_mv = sem("mean_var_done")
        a_sd = sem("std_done")
        v_rs = sem("rstd_done")
        v_xn = sem("x_normed")
        p_col = sem("shift_column_set")
        p_delta = sem("delta_done")
        v_mx0 = sem("mix0_done")
        p_add = sem("mixed")
        a_th = sem("gate_tanh_done")
        a_d = sem("decay_set")
        pe_r = sem("r_ready")
        v_ruk = sem("ruk_done")
        p_bv = sem("bonus_done")
        vb_in = [sem(f"v_spread{i}") for i in range(VRING)]
        p_kv = sem("kv_done")
        v_c = sem("state_column_set")
        v_scan = sem("scanned")
        v_p = sem("products_done")
        pe_red = sem("heads_reduced")
        v_ob = sem("o_summed")
        a_sq = sem("o_squared")
        v_rg = sem("o_rstd_done")
        v_on = sem("o_normed")
        a_y = sem("o_scaled")
        p_y = sem("o_gated")
        v_h2 = sem("h_attn_summed")
        v_st2 = sem("stats2_done")
        v_mv2 = sem("mean_var2_done")
        a_sd2 = sem("std2_done")
        v_rs2 = sem("rstd2_done")
        v_yn = sem("y_normed")
        p_hb = sem("bias_added")

        NWEIGHTS = 15
        block = ctx.enter_context(nc.Block())

        def emptied(eng, b, name):
            wait(eng, free[BANK[name]], b.fill(name))

        def filled(eng, b, name):
            wait(eng, full[BANK[name]], b.fill(name))
            return W[BANK[name]]

        def take_wait(ops, cells, taken):
            taken.append(len(taken) + 1)
            ops.tensor_tensor(cells[:, taken[-1]:taken[-1] + 1], cells[:, 0:1], cells[:, 0:1], ALU.add)

        @block.sync
        def _(sp):
            for dst, src in ((vec_s[:, :], vecs), (bt_s[0:RANK, :], b_tok), (bt_s[P // TC:P // TC + RANK, :], b_tok),
                             (wx1_s[:, :, :], wx1.rearrange("(k p) n -> p k n", p=P)),
                             (wx2_s[:, :], wx2[0:P, :]), (wx2g_s[RLO:2 * RLO, :], wx2[P:P + RLO, :]),
                             (ww1_s[:, :, :], ww1.rearrange("(k p) n -> p k n", p=P)), (ww2_s[:, :], ww2),
                             (wk_s[:, :, :], wk.rearrange("(k p) n -> p k n", p=P)),
                             (wv_s[:, :, :], wv.rearrange("(k p) n -> p k n", p=P)),
                             (wg_s[:, :, :], wg.rearrange("(k p) n -> p k n", p=P)),
                             (wr_s[:, :, :], wr.rearrange("(k p) n -> p k n", p=P)),
                             (wo_s[:, :, :], wo.rearrange("(k p) n -> p k n", p=P)),
                             (wf, w_ffn.rearrange("(k p) n -> p k n", p=P)),
                             (bias_s[:, :], b_ffn.to_broadcast([P, D]))):
                sp.dma_start(dst, src).then_inc(w_in, 16)

            def load_idx(b, _):
                q = b.off % 4
                src = x[bass.ds(sp.snap(b.times(1)), 1), :, :].rearrange("b p c -> (b p) c") if b.turn is not None else x[b.off, :, :]
                wait(sp, idx_st, b.times(3, 3 - 12))
                sp.dma_start(idx_i[:, q, :], src).then_inc(idx_in[q], 16)

            def spread(b, v):
                if v == 0:
                    emptied(sp, b, "pv1")
                else:
                    wait(sp, p_kv, b.times(HV, v + 2 - VRING))
                for hh in range(HH):
                    r0 = NH * (v % VG) + NH // HH * hh
                    sp.dma_start(vB[:, v % VRING, hh, :],
                                 vT[r0:r0 + NH // HH, b.off % 2, v // VG:v // VG + 1, :].to_broadcast([NH // HH, HK, TB]))\
                        .then_inc(vb_in[v % VRING], 16)

            whole_run(sp, {"sp_idx": load_idx, "sp_spread": spread})

        @block.gpsimd
        def _(pool):
            pool_taken = []
            nc.gpsimd.memset(pool_cell[:, :], 0.0).then_inc(c_cell[0], 1)
            pool.wait_ge(c_cell[0], 1)
            nc.gpsimd.memset(ident[:, :], 0.0).then_inc(c_sel, 1)
            nc.gpsimd.memset(head_sel[:, :, :, :], 1.0).then_inc(c_sel, 1)
            nc.gpsimd.memset(head_mean[:, :, :], 0.0).then_inc(c_sel, 1)
            nc.gpsimd.memset(eps_s[:, :], EPS).then_inc(c_sel, 1)
            nc.gpsimd.memset(ag[:, :, :, :], 0.0).then_inc(c_sel, 1)
            pool.wait_ge(c_sel, 5)
            count = 5
            nc.gpsimd.affine_select(out=ident[:, :], in_=ident[:, :], compare_op=ALU.not_equal, fill=1.0, base=0,
                                    pattern=[[-1, P]], channel_multiplier=1).then_inc(c_k, 1)
            for hh in range(HH):
                nc.gpsimd.affine_select(out=head_sel[:, hh, :, :], in_=head_sel[:, hh, :, :], compare_op=ALU.is_ge, fill=0.0,
                                        base=HK * NH // HH * hh, pattern=[[0, VG], [-HK, NH]], channel_multiplier=1).then_inc(c_sel, 1)
                count += 1
                pool.wait_ge(c_sel, count)
                nc.gpsimd.affine_select(out=head_sel[:, hh, :, :], in_=head_sel[:, hh, :, :], compare_op=ALU.is_ge, fill=0.0,
                                        base=HK - 1 - HK * NH // HH * hh, pattern=[[0, VG], [HK, NH]], channel_multiplier=-1).then_inc(c_k, 1)
            for vi in range(VG):
                ins = nc.gpsimd.affine_select(out=head_mean[:, :, :], in_=head_mean[:, :, :], compare_op=ALU.not_equal, fill=1.0 / HV,
                                              base=-NH * vi, pattern=[[0, VG], [-1, NH]], channel_multiplier=1)
                if vi < VG - 1:
                    ins.then_inc(c_sel, 1)
                    count += 1
                    pool.wait_ge(c_sel, count)
                else:
                    ins.then_inc(c_k, 1)

            def gather(b, _):
                q = b.off % 4
                wait(pool, stored[q], b.round(4, 16))
                wait(pool, idx_st, b.times(3, 3))
                take_wait(nc.gpsimd, pool_cell, pool_taken)
                for c in range(TC):
                    nc.gpsimd.indirect_dma_start(h[:, q, c, :], None, w_tok, bass.IndirectOffsetOnAxis(ap=idx_u[:, q, c:c + 1], axis=0))\
                        .then_inc(rows_in[q], 16)
                    nc.gpsimd.indirect_dma_start(ag[:, q, c, 0:RANK], None, a_tok, bass.IndirectOffsetOnAxis(ap=idx_u[:, q, c:c + 1], axis=0))\
                        .then_inc(rows_in[q], 16)

            def shift_difference(n, _):
                q = n.off % 2
                emptied(pool, n, "xT1")
                take_wait(nc.gpsimd, pool_cell, pool_taken)
                if n.off % PER_SEQ == 0:
                    nc.gpsimd.memset(xT[:, q, :, 0:1], 0.0).then_inc(p_col, 1)
                else:
                    nc.gpsimd.tensor_copy(xT[:, q, :, 0:1], xT[:, 1 - q, :, TB:TB + 1]).then_inc(p_col, 1)
                if n.off > 0:
                    emptied(pool, n + -1, "mu4b")
                pool.wait_ge(p_col, n.times(1, 1))
                nc.gpsimd.tensor_tensor(delta[:, :, :], xT[:, q, :, 0:TB], xT[:, q, :, 1:TB + 1], ALU.subtract).then_inc(p_delta, 1)

            def mix_add(n, a):
                emptied(pool, n, f"mu{a}b")
                m = mx[:, (1 + a) % MXRING, :, :]
                nc.gpsimd.tensor_tensor(m, m, xT[:, n.off % 2, :, 1:TB + 1], ALU.add).then_inc(p_add, 1)

            def key_value(j, v):
                if v == 0:
                    emptied(pool, j, "pk")
                if v % 2 == 0:
                    wait(pool, v_scan, j.times(HV, v + 2 - KVRING))
                wait(pool, vb_in[v % VRING], j.times(32 * HV // VRING, 32 * (v // VRING + 1)))
                nc.gpsimd.tensor_tensor(kv[:, v % KVRING, :, :], vB[:, v % VRING, :, :], kT[:, j.off % 2, :, :], ALU.mult)\
                    .then_inc(p_kv, 1)

            def bonus(j, _):
                emptied(pool, j, "pv1")
                wait(pool, v_ob, j.times(2))
                emptied(pool, j, "bs")
                nc.gpsimd.tensor_tensor(bv[:, :, :], vT[:, j.off % 2, :, :],
                                        bsb[:, :].rearrange("p (m t) -> p m t", m=1).to_broadcast([P, VT, TB]), ALU.mult)\
                    .then_inc(p_bv, 1)

            def gated(t, _):
                wait(pool, a_y, t.times(1, 1))
                nc.gpsimd.tensor_tensor(yT[:, :, :], yT[:, :, :], gate[:, t.off % 2, :, :], ALU.mult).then_inc(p_y, 1)

            def add_bias(t, _):
                wait(pool, v_yn, t.times(1, 1))
                q = t.off % 4
                nc.gpsimd.tensor_tensor(h[:, q, :, :], h[:, q, :, :],
                                        bias_s[:, :].rearrange("p (c d) -> p c d", c=1).to_broadcast([P, TC, D]), ALU.add)\
                    .then_inc(p_hb, 1)

            whole_run(pool, {"gp_gather": gather, "gp_delta": shift_difference, "gp_add": mix_add, "gp_kv": key_value,
                             "gp_bonus": bonus, "gp_gate": gated, "gp_bias": add_bias})

        @block.scalar
        def _(act):
            act.wait_ge(w_in, 16 * NWEIGHTS)
            act.wait_ge(c_sel, 5)
            nc.scalar.mul(gn_half[:, :], vec_s[:, NC_GW:NC_GW + 2 * VT], 0.5).then_inc(c_k, 1)

            def take(b, name, dst, src, func=ACT.Copy, last=True, **more):
                w = filled(act, b, name)
                ins = nc.scalar.activation(dst, src(w), func, **more)
                if last:
                    ins.then_inc(free[BANK[name]], 1)

            def lora_rows(n, _):
                take(n, "agT", agT[:, :], lambda w: w[:, 0:P])

            def deviation1(n, _):
                wait(act, v_mv, n.times(1, 1))
                nc.scalar.activation(sd[:, 0, :], mv[:, 0, :, 1], ACT.Sqrt, bias=eps_s[:, 0:1]).then_inc(a_sd, 1)

            def deviation2(t, _):
                wait(act, v_mv2, t.times(1, 1))
                nc.scalar.activation(sd[:, 1, :], mv[:, 1, :, 1], ACT.Sqrt, bias=eps_s[:, 0:1]).then_inc(a_sd2, 1)

            def x_turned(n, i):
                if i == 0:
                    wait(act, p_add, n.times(5, -5))
                    wait(act, p_col, n.times(1))
                take(n, f"xT{i}", xT[:, n.off % 2, 2 * i:2 * i + 2, 1:TB + 1].rearrange("p f (t c) -> p f t c", c=TC),
                     lambda w: w[:, :].rearrange("p (f c t) -> p f t c", f=2, c=TC))

            def z_tanh(n, _):
                take(n, "z", z0[:, :], lambda w: w[:, 0:TB], ACT.Tanh, last=False)
                take(n, "z", z1[RLO:2 * RLO, :], lambda w: w[RLO:2 * RLO, TB:2 * TB], ACT.Tanh)

            def decay_tanh(n, _):
                take(n, "pw", t2[:, :], lambda w: w[0:GLO, 0:TB], ACT.Tanh)

            def decay_exp(n, _):
                w = filled(act, n, "w2")
                for hh in range(HH):
                    ins = nc.scalar.activation(ew[:, hh, :], w[:, hh * TB:hh * TB + TB], ACT.Exp,
                                               bias=vec_s[:, NC_BW + hh:NC_BW + hh + 1])
                ins.then_inc(free[BANK["w2"]], 1)

            def decay(n, _):
                emptied(act, n, "w2")
                wait(act, v_scan, n.times(HV))
                nc.scalar.activation(DK[:, :], ew[:, :, :].rearrange("p a t -> p (a t)"), ACT.Exp, scale=-1.0).then_inc(a_d, 1)

            def k_out(n, _):
                wait(act, p_kv, n.times(HV, -HV))
                wait(act, v_ruk, n.times(1, -1))
                take(n, "pk", kT[:, n.off % 2, :, :], lambda w: w[:, :].rearrange("p (a t) -> p a t", a=HH))

            def v_out(n, i):
                if i == 0:
                    wait(act, p_kv, n.times(HV, -HV))
                    wait(act, p_bv, n.times(1, -1))
                take(n, f"pv{i}", vT[:, n.off % 2, 2 * i:2 * i + 2, :], lambda w: w[:, :].rearrange("p (m t) -> p m t", m=2))

            def gate_tanh(n, i):
                if i == 0:
                    wait(act, p_y, n.times(1, -1))
                w = filled(act, n, f"pg{i}")
                nc.scalar.activation(gate[:, n.off % 2, 2 * i:2 * i + 2, :], w[:, :].rearrange("p (m t) -> p m t", m=2),
                                     ACT.Tanh, scale=0.5).then_inc(a_th, 1)

            def bonus_sums(j, _):
                wait(act, p_bv, j.times(1))
                take(j, "bs", bsb[:, :], lambda w: w[:, 0:TB])

            def squares(t, _):
                wait(act, v_ob, t.times(2, 2))
                if t.off > 0:
                    filled(act, t + -1, "f1")
                nc.scalar.activation(sq, ob[:, t.off % 2, :, :], ACT.Square).then_inc(a_sq, 1)

            def deviation_o(t, _):
                wait(act, v_rg, t.times(1))
                take(t, "var", sdo[:, :], lambda w: w[:, 0:TB], ACT.Sqrt, bias=eps_s[:, 0:1])

            def scaled(t, _):
                wait(act, v_on, t.times(1, 1))
                if t.off > 0:
                    filled(act, t + -1, "wo1")
                for m in range(VT):
                    ins = nc.scalar.activation(yT[:, m, :], ob[:, t.off % 2, m, :], ACT.Identity,
                                               bias=gn_half[:, VT + m:VT + m + 1], scale=gn_half[:, m:m + 1])
                ins.then_inc(a_y, 1)

            def y_turned(t, i):
                take(t, f"yT{i}", y2T[:, 2 * i:2 * i + 2, :, :], lambda w: w[:, :].rearrange("p (f c t) -> p f c t", f=2, c=TC))

            def store(t, _):
                at = bass.ds(t.times(1), 1) if t.turn is not None else slice(t.off, t.off + 1)
                emptied(act, t, "f1")
                act.dma_start(out[at, :, :].rearrange("b p n -> (b p) n"), h[:, t.off % 4, :, :].rearrange("p c d -> p (c d)"))\
                    .then_inc(stored[t.off % 4], 16)

            whole_run(act, {"act_agT": lora_rows, "act_sd1": deviation1, "act_sd2": deviation2, "act_xT": x_turned, "act_z": z_tanh,
                            "act_t2": decay_tanh, "act_ew": decay_exp, "act_d": decay, "act_k": k_out, "act_v": v_out,
                            "act_th": gate_tanh, "act_bs": bonus_sums, "act_sq": squares, "act_sdo": deviation_o,
                            "act_y": scaled, "act_yT": y_turned, "act_store": store})
            for q in range(4):
                act.wait_ge(stored[q], 16 * (NBLK // 4))

        @block.vector
        def _(dve):
            dve_taken = []
            nc.vector.memset(dve_cell[:, :], 0.0).then_inc(c_cell[1], 1)
            dve.wait_ge(c_cell[1], 1)
            dve.wait_ge(w_in, 16 * NWEIGHTS)
            nc.vector.tensor_reduce(wv_mean, wv_s[:, :, :].rearrange("p k (v h) -> p k h v", v=HV), AX.X, ALU.add).then_inc(c_v, 1)
            dve.wait_ge(c_v, 1)
            for v in range(HV):
                nc.vector.scalar_tensor_tensor(wv_s[:, :, v * NH:v * NH + NH], wv_mean, -1.0 / HV, wv_s[:, :, v * NH:v * NH + NH],
                                               ALU.mult, ALU.add).then_inc(c_v, 1)
            nc.vector.tensor_reduce(alpha[:, :], wf, AX.X, ALU.add, apply_absolute_value=True).then_inc(c_f, 1)
            dve.wait_ge(c_f, 1)
            nc.vector.tensor_scalar(alpha[:, :], alpha[:, :], 1.0 / D, None, ALU.mult).then_inc(c_f, 1)
            nc.vector.tensor_scalar(bw, wf, 0.0, 2.0, ALU.is_ge, ALU.mult).then_inc(c_f, 1)
            dve.wait_ge(c_f, 3)
            for f in range(KD):
                nc.vector.tensor_scalar(bw[:, f, :], bw[:, f, :], -1.0, alpha[:, f:f + 1], ALU.add, ALU.mult).then_inc(c_f, 1)
            dve.wait_ge(c_f, 3 + KD)
            nc.vector.tensor_tensor(bw, bw, wf, ALU.subtract).then_inc(c_f, 1)
            dve.wait_ge(c_f, 4 + KD)
            nc.vector.tensor_tensor(bw, bw, wf, ALU.add).then_inc(c_f, 1)
            for f in range(KD):
                dve.wait_ge(c_ft, f + 1)
                nc.vector.tensor_copy(wf_s[:, f, :], W[f][:, :]).then_inc(c_fc, 1)

            def layer_stats(b, k, stats_sem, mv_sem, done):
                q = b.off % 4
                wait(dve, done, b.times(1))
                for c in range(TC):
                    ins = nc.vector.bn_stats(stats[:, k, c, :], h[:, q, c, :])
                ins.then_inc(stats_sem, 1)
                dve.wait_ge(stats_sem, b.times(1, 1))
                take_wait(nc.vector, dve_cell, dve_taken)
                for c in range(TC):
                    ins = nc.vector.bn_aggr(mv[:, k, c, :], stats[:, k, c, :])
                ins.then_inc(mv_sem, 1)

            def layer_norm(b, k, sd_sem, rs_sem, done):
                q = b.off % 4
                dve.wait_ge(sd_sem, b.times(1, 1))
                nc.vector.reciprocal(rs[:, k, :], sd[:, k, :]).then_inc(rs_sem, 1)
                dve.wait_ge(rs_sem, b.times(1, 1))
                for c in range(TC):
                    ins = nc.vector.tensor_scalar(xn[:, c, :], h[:, q, c, :], mv[:, k, c, 0:1], rs[:, k, c:c + 1],
                                                  ALU.subtract, ALU.mult)
                ins.then_inc(done, 1)

            def clamp_idx(b, _):
                q = b.off % 4
                wait(dve, idx_in[q], b.round(4, 16, 16))
                wait(dve, idx_st, b.times(3))
                wait(dve, rows_in[q], b.round(4, 64))
                nc.vector.tensor_scalar(idx_f[:, 0, :], idx_i[:, q, :], float(VOCAB - 1), float(-VOCAB), ALU.min, ALU.max).then_inc(idx_st, 1)
                dve.wait_ge(idx_st, b.times(3, 1))
                nc.vector.tensor_scalar(idx_f[:, 1, :], idx_f[:, 0, :], 0.0, float(VOCAB), ALU.is_lt, ALU.mult).then_inc(idx_st, 1)
                dve.wait_ge(idx_st, b.times(3, 2))
                nc.vector.tensor_tensor(idx_u[:, q, :], idx_f[:, 0, :], idx_f[:, 1, :], ALU.add).then_inc(idx_st, 1)

            def add_fill(b, name, c):
                w = filled(dve, b, name)
                hc = h[:, b.off % 4, c, :]
                nc.vector.tensor_tensor(hc, hc, w[:, :], ALU.add).then_inc(free[BANK[name]], 1)

            def add_lora(n, c):
                add_fill(n, f"lora{c}", c)

            def add_attention(t, c):
                add_fill(t, f"wo{c}", c)

            def add_ffn(t, c):
                if c == 0:
                    dve.wait_ge(p_hb, t.times(1, 1))
                add_fill(t, f"f{c}", c)

            def stats1(n, _):
                emptied(dve, n, "lora1")
                layer_stats(n, 0, v_st, v_mv, v_xn)

            def stats2(t, _):
                emptied(dve, t, "wo1")
                layer_stats(t, 1, v_st2, v_mv2, v_yn)

            def norm1(n, _):
                if n.off + Y_TURNED_BEFORE >= 0:
                    filled(dve, n + Y_TURNED_BEFORE, "yT1")
                layer_norm(n, 0, a_sd, v_rs, v_xn)

            def norm2(t, _):
                if t.off + X_TURNED_BEFORE < NBLK:
                    filled(dve, t + X_TURNED_BEFORE, "xT1")
                layer_norm(t, 1, a_sd2, v_rs2, v_yn)

            def mix0(n, _):
                if n.off > 0:
                    filled(dve, n + -1, "pv1")
                dve.wait_ge(p_delta, n.times(1, 1))
                for f in range(KD):
                    ins = nc.vector.scalar_tensor_tensor(mx[:, 0, f, :], delta[:, f, :], vec_s[:, NC_MU + f:NC_MU + f + 1],
                                                         xT[:, n.off % 2, f, 1:TB + 1], ALU.mult, ALU.add)
                ins.then_inc(v_mx0, 1)

            def mix_times_delta(n, part):
                a, i = part // 2, part % 2
                if i == 0:
                    if a == 0 and n.off > 0:
                        filled(dve, n + -1, "pg1")
                    if a == 1:
                        wait(dve, pe_r, n.times(1))
                    if a >= 2:
                        filled(dve, n, ("z", "pw", "pk")[a - 2])
                name = f"mu{a}{'ab'[i]}"
                w = filled(dve, n, name)
                nc.vector.tensor_tensor(mx[:, (1 + a) % MXRING, 2 * i:2 * i + 2, :], w[:, :].rearrange("p (f t) -> p f t", f=2),
                                        delta[:, 2 * i:2 * i + 2, :], ALU.mult).then_inc(free[BANK[name]], 1)

            def gate_mult(n, i):
                dve.wait_ge(a_th, n.times(2, i + 1))
                gt = gate[:, n.off % 2, 2 * i:2 * i + 2, :]
                nc.vector.scalar_tensor_tensor(gt, gt, 1.0, W[BANK[f"pg{i}"]][:, :].rearrange("p (m t) -> p m t", m=2), ALU.add, ALU.mult)\
                    .then_inc(free[BANK[f"pg{i}"]], 1)

            def scan(j, v):
                if v % VG == 0:
                    wait(dve, pe_red, j.times(VT, v // VG + 1 - VT))
                    if j.off % PER_SEQ == 0:
                        nc.vector.memset(state[:, v:v + VG, :, 0:1], 0.0).then_inc(v_c, 1)
                    else:
                        nc.vector.tensor_copy(state[:, v:v + VG, :, 0:1], state[:, v:v + VG, :, TB:TB + 1]).then_inc(v_c, 1)
                    dve.wait_ge(v_c, j.times(VT, v // VG + 1))
                if v == 0:
                    dve.wait_ge(a_d, j.times(1, 1))
                dve.wait_ge(p_kv, j.times(HV, v + 1))
                for hh in range(HH):
                    ins = nc.vector.tensor_tensor_scan(state[:, v, hh, 1:TB + 1], d_t[:, hh, :], kv[:, v % KVRING, hh, :],
                                                       state[:, v, hh, 0:1], ALU.mult, ALU.add)
                ins.then_inc(v_scan, 1)

            def products(j, v):
                dve.wait_ge(v_scan, j.times(HV, v + 1))
                if v == 0:
                    dve.wait_ge(pe_r, j.times(1, 1))
                nc.vector.tensor_tensor(state[:, v, :, 0:TB], state[:, v, :, 0:TB], r_t, ALU.mult).then_inc(v_p, 1)

            def bonus_product(j, _):
                emptied(dve, j, "pk")
                dve.wait_ge(pe_r, j.times(1, 1))
                for hh in range(HH):
                    ins = nc.vector.scalar_tensor_tensor(ruk[:, hh, :], r_t[:, hh, :], vec_s[:, NC_U + hh:NC_U + hh + 1],
                                                         kT[:, j.off % 2, hh, :], ALU.mult, ALU.mult)
                ins.then_inc(v_ruk, 1)

            def sum_o(j, i):
                wait(dve, a_y, j.times(1, -1))
                dve.wait_ge(p_bv, j.times(1, 1))
                dve.wait_ge(pe_red, j.times(VT, 2 * i + 2))
                nc.vector.tensor_tensor(ob[:, j.off % 2, 2 * i:2 * i + 2, :], bv[:, 2 * i:2 * i + 2, :],
                                        O[i][:, :].rearrange("p (m t) -> p m t", m=2), ALU.add).then_inc(v_ob, 1)

            def normalise(t, _):
                wait(dve, v_on, t.times(1))
                emptied(dve, t, "var")
                nc.vector.reciprocal(rg[:, :], sdo[:, :]).then_inc(v_rg, 1)
                dve.wait_ge(v_rg, t.times(1, 1))
                o = ob[:, t.off % 2, :, :]
                nc.vector.tensor_tensor(o, o, rg[:, :].rearrange("p (m t) -> p m t", m=1).to_broadcast([P, VT, TB]), ALU.mult)\
                    .then_inc(v_on, 1)

            whole_run(dve, {"dv_idx": clamp_idx, "dv_lora": add_lora, "dv_st1": stats1, "dv_n1": norm1, "dv_mix0": mix0,
                            "dv_mus": mix_times_delta, "dv_gate": gate_mult, "dv_scan": scan, "dv_prod": products,
                            "dv_ruk": bonus_product, "dv_ob": sum_o, "dv_on": normalise,
                            "dv_h2": add_attention, "dv_st2": stats2, "dv_n2": norm2, "dv_out": add_ffn})

        @block.tensor
        def _(pe):
            pe.wait_ge(w_in, 16 * NWEIGHTS)
            pe.wait_ge(c_k, 5)
            pe.wait_ge(c_v, 1 + HV)
            pe.wait_ge(c_f, 5 + KD)
            for f in range(KD):
                for o in range(KD):
                    ins = nc.tensor.transpose(W[f][:, o * P:o * P + P],
                                              bw[:, o, f * P:f * P + P], ident[:, :])
                ins.then_inc(c_ft, 1)
            pe.wait_ge(c_fc, KD)

            def fill(b, name):
                wait(pe, free[BANK[name]], b.fill(name, -1))
                return W[BANK[name]], full[BANK[name]]

            def project(w, bank, src, m, cols=P, **place):
                for k in range(KD):
                    ins = nc.tensor.matmul(bank, w[:, k, m * P:m * P + cols], src[:, k, :], start=(k == 0), stop=(k == KD - 1), **place)
                return ins

            def turn(w, src, i):
                for g in range(2):
                    for c in range(TC):
                        ins = nc.tensor.transpose(w[:, (2 * g + c) * P:(2 * g + c + 1) * P],
                                                  src[:, c, (2 * i + g) * P:(2 * i + g + 1) * P], ident[:, :])
                return ins

            def lora_turn(n, _):
                q = n.off % 4
                wait(pe, rows_in[q], n.round(4, 64, 64))
                w, f = fill(n, "agT")
                nc.tensor.transpose(w[:, 0:P], ag[:, q, :, :].rearrange("p c r -> p (c r)"), ident[:, :]).then_inc(f, 1)

            def lora(n, _):
                emptied(pe, n, "agT")
                banks = [fill(n, f"lora{c}") for c in range(TC)]
                for c, (w, f) in enumerate(banks):
                    r0 = P // TC * c
                    nc.tensor.matmul(w[:, :], agT[r0:r0 + RANK, :], bt_s[r0:r0 + RANK, :], start=True, stop=True,
                                     tile_position=(r0, 0)).then_inc(f, 1)

            def turn_x(n, i):
                pe.wait_ge(v_xn, n.times(1, 1))
                w, f = fill(n, f"xT{i}")
                turn(w, xn, i).then_inc(f, 1)

            def turn_y(t, i):
                pe.wait_ge(v_yn, t.times(1, 1))
                w, f = fill(t, f"yT{i}")
                turn(w, xn, i).then_inc(f, 1)

            def token_shift_rank(n, _):
                pe.wait_ge(v_mx0, n.times(1, 1))
                w, f = fill(n, "z")
                project(wx1_s, w[:, 0:TB], mx[:, 0, :, :], 0)
                project(wx1_s, w[RLO:2 * RLO, TB:2 * TB], mx[:, 0, :, :], 1, RLO, tile_position=(0, RLO)).then_inc(f, 1)

            def mus(n, part):
                emptied(pe, n, "z")
                i = part % 2
                mixes = (0, 1, 2) if part < 2 else (3, 4)
                banks = [fill(n, f"mu{a}{'ab'[i]}") for a in mixes]
                for g in range(2):
                    f0 = (2 * i + g) * P
                    for a, (w, f) in zip(mixes, banks):
                        r0 = RLO * MIXES[a]
                        w2, zz = (wx2g_s[RLO:2 * RLO, :], z1[RLO:2 * RLO, :]) if MIXES[a] == MIX_G else (wx2_s[r0:r0 + RLO, :], z0[r0:r0 + RLO, :])
                        ins = nc.tensor.matmul(w[:, g * TB:g * TB + TB], w2[:, f0:f0 + P], zz, start=True, stop=True)
                        if g == 1:
                            ins.then_inc(f, 1)

            def mixed(n, a):
                pe.wait_ge(p_add, n.times(5, a + 1))
                return mx[:, (1 + a) % MXRING, :, :]

            def proj(n, a):
                src = mixed(n, a)
                if MIXES[a] == MIX_W:
                    w, f = fill(n, "pw")
                    project(ww1_s, w[0:GLO, 0:TB], src, 0, GLO).then_inc(f, 1)
                if MIXES[a] == MIX_K:
                    w, f = fill(n, "pk")
                    for hh in range(HH):
                        ins = project(wk_s, w[:, hh * TB:hh * TB + TB], src, hh)
                    ins.then_inc(f, 1)
                if MIXES[a] == MIX_R:
                    wait(pe, v_p, n.times(HV))
                    for hh in range(HH):
                        ins = project(wr_s, R[:, hh * TB:hh * TB + TB], src, hh)
                    ins.then_inc(pe_r, 1)

            def proj_v(n, i):
                src = mixed(n, MIXES.index(MIX_V))
                w, f = fill(n, f"pv{i}")
                for g in range(2):
                    ins = project(wv_s, w[:, g * TB:g * TB + TB], src, 2 * i + g)
                ins.then_inc(f, 1)

            def proj_g(n, i):
                src = mixed(n, MIXES.index(MIX_G))
                w, f = fill(n, f"pg{i}")
                for g in range(2):
                    ins = project(wg_s, w[:, g * TB:g * TB + TB], src, 2 * i + g)
                ins.then_inc(f, 1)

            def decay_rank(n, _):
                emptied(pe, n, "pw")
                w, f = fill(n, "w2")
                for hh in range(HH):
                    ins = nc.tensor.matmul(w[:, hh * TB:hh * TB + TB], ww2_s[:, hh * P:hh * P + P], t2[:, :], start=True, stop=True)
                ins.then_inc(f, 1)

            def bonus_sum(j, _):
                pe.wait_ge(v_ruk, j.times(1, 1))
                w, f = fill(j, "bs")
                for hh in range(HH):
                    ins = nc.tensor.matmul(w[:, 0:TB], head_sel[:, hh, :, :].rearrange("p v h -> p (v h)"), ruk[:, hh, :],
                                           start=(hh == 0), stop=(hh == HH - 1))
                ins.then_inc(f, 1)

            def reduce_heads(j, m):
                if m % 2 == 0:
                    wait(pe, v_ob, j.times(2, m // 2 - 1))
                pe.wait_ge(v_p, j.times(HV, VG * (m + 1)))
                for hh in range(HH):
                    for vi in range(VG):
                        ins = nc.tensor.matmul(O[m // 2][NH * vi:NH * vi + NH, (m % 2) * TB:(m % 2) * TB + TB],
                                               head_sel[:, hh, 0, :], state[:, VG * m + vi, hh, 0:TB],
                                               start=(hh == 0), stop=(hh == HH - 1), tile_position=(0, NH * vi))
                ins.then_inc(pe_red, 1)

            def variance(t, _):
                pe.wait_ge(a_sq, t.times(1, 1))
                w, f = fill(t, "var")
                for m in range(VT):
                    ins = nc.tensor.matmul(w[:, 0:TB], head_mean[:, :, :].rearrange("p v h -> p (v h)"), sq[:, m, :],
                                           start=(m == 0), stop=(m == VT - 1))
                ins.then_inc(f, 1)

            def proj_o(t, c):
                pe.wait_ge(p_y, t.times(1, 1))
                w, f = fill(t, f"wo{c}")
                for m in range(VT):
                    ins = nc.tensor.matmul(w[:, :], yT[:, m, c:TB:TC], wo_s[:, m, :], start=(m == 0), stop=(m == VT - 1))
                ins.then_inc(f, 1)

            def ffn(t, c):
                emptied(pe, t, "yT1")
                w, f = fill(t, f"f{c}")
                for k in range(KD):
                    ins = nc.tensor.matmul(w[:, :], y2T[:, k, c, :], wf_s[:, k, :], start=(k == 0), stop=(k == KD - 1))
                ins.then_inc(f, 1)

            whole_run(pe, {"pe_agT": lora_turn, "pe_lora": lora, "pe_xT": turn_x, "pe_yT": turn_y, "pe_z": token_shift_rank,
                           "pe_mus": mus, "pe_proj": proj, "pe_pv": proj_v, "pe_pg": proj_g, "pe_w2": decay_rank,
                           "pe_bs": bonus_sum, "pe_red": reduce_heads, "pe_var": variance, "pe_wo": proj_o,
                           "pe_ffn": ffn})


_ORDER = ["x", "w_tok", "a_tok", "b_tok", "vecs", "wx1", "wx2", "wr", "ww1", "ww2", "wk", "wv", "wg", "wo", "w_ffn", "b_ffn"]


def kernel(x, L0_tok_W, L0_tok_A, L0_tok_B, L0_attn_mu_x, L0_attn_Wx1, L0_attn_Wx2, L0_attn_Wr, L0_attn_Ww1, L0_attn_Ww2,
           L0_attn_bw, L0_attn_Wk, L0_attn_Wv, L0_attn_Wg, L0_attn_bonus, L0_attn_gn_w, L0_attn_gn_b, L0_attn_Wo,
           L0_ffn_weight, L0_ffn_bias):
    import numpy as np
    from concourse import bacc
    from concourse.bass_utils import run_bass_kernel_spmd

    def columns(v):
        return np.asarray(v).reshape(-1, P).T

    def value_major(w):
        return np.asarray(w).reshape(-1, NH, HV).transpose(0, 2, 1).reshape(-1, D)

    gn = [columns(np.repeat(np.asarray(v), NH)) for v in (L0_attn_gn_w, L0_attn_gn_b)]
    given = {
        "x": np.asarray(x).reshape(NBLK, P, TC),
        "w_tok": L0_tok_W, "a_tok": L0_tok_A, "b_tok": L0_tok_B,
        "vecs": np.concatenate([columns(L0_attn_mu_x), columns(L0_attn_bonus), columns(L0_attn_bw)] + gn, axis=1),
        "wx1": L0_attn_Wx1, "wx2": np.asarray(L0_attn_Wx2).reshape(5 * RLO, D), "wr": L0_attn_Wr, "ww1": L0_attn_Ww1,
        "ww2": L0_attn_Ww2, "wk": L0_attn_Wk, "wv": value_major(L0_attn_Wv), "wg": value_major(L0_attn_Wg),
        "wo": value_major(np.asarray(L0_attn_Wo).T).T, "w_ffn": L0_ffn_weight, "b_ffn": np.asarray(L0_ffn_bias).reshape(1, D),
    }
    nc = bacc.Bacc("TRN2", target_bir_lowering=False, num_devices=1)
    arrays, args = {}, []
    for name in _ORDER:
        a = np.ascontiguousarray(given[name])
        arrays[f"in_{name}"] = a
        args.append(nc.dram_tensor(f"in_{name}", a.shape, mybir.dt.from_np(a.dtype), kind="ExternalInput").ap())
    args.append(nc.dram_tensor("out_h", (NBLK, P, TC * D), F32, kind="ExternalOutput").ap())
    tower_kernel(nc, *args)
    r = run_bass_kernel_spmd(nc, [arrays], core_ids=[0])
    return r.results[0]["out_h"].reshape(SEQS, SEQ, D)
```

```python
from contextlib import ExitStack

import concourse.bass as bass
from concourse import mybir

F32 = mybir.dt.float32
F32R = mybir.dt.float32r
I32 = mybir.dt.int32
U32 = mybir.dt.uint32
ALU = mybir.AluOpType
ACT = mybir.ActivationFunctionType
AX = mybir.AxisListType

P = 128
SEQS, SEQ = 8, 1024
D = 512
KD = D // P
NH, HK, HV = 32, 8, 16
VG = 4
VT = HV // VG
HH = 2
RLO, GLO = 32, 64
RANK = 16
VOCAB = 32000
EPS = 1e-5
TB = 256
TC = TB // P
NBLK = SEQS * SEQ // TB
PER_SEQ = SEQ // TB
LOOPED = 4
VRING, KVRING, MXRING = 8, 4, 3
MIX_R, MIX_W, MIX_K, MIX_V, MIX_G = range(5)
MIXES = [MIX_W, MIX_K, MIX_V, MIX_G, MIX_R]
NC_MU, NC_U, NC_BW, NC_GW, NC_GB, NC_FB = 0, 4, 6, 8, 12, 16
NW = 4

SCHEDULE = [
    ("dv_gate", 1, -2), ("act_yT", 0, -3), ("sp_spread", 12, -2), ("dv_yl", 0, -3), ("pe_red", 0, -2), ("act_zr", 1, -1),
    ("act_yT", 1, -3), ("dv_yl", 1, -3), ("pe_mus", 0, -1), ("gp_kv", 12, -2), ("dv_scan", 10, -2), ("dv_mus", 0, -1),
    ("sp_spread", 13, -2), ("dv_mus", 1, -1), ("pe_ffn", 0, -3), ("gp_kv", 13, -2), ("pe_mus", 1, -1), ("act_f", 0, -3),
    ("dv_scan", 11, -2), ("dv_mus", 2, -1), ("gp_add", 0, -1), ("dv_mus", 3, -1), ("sp_spread", 14, -2), ("dv_prod", 9, -2),
    ("dv_scan", 12, -2), ("pe_ffn", 1, -3), ("pe_mus", 2, -1), ("act_f", 1, -3), ("dv_mus", 4, -1), ("pe_red", 1, -2),
    ("pe_fT", 0, -3), ("gp_add", 1, -1), ("dv_mus", 5, -1), ("dv_prod", 10, -2), ("dv_scan", 13, -2), ("dv_out", 0, -3),
    ("pe_proj", 0, -1), ("pe_fT", 1, -3), ("dv_out", 1, -3), ("pe_proj", 1, -1), ("sp_spread", 15, -2), ("act_t2", 0, -1),
    ("act_store", 0, -3), ("gp_kv", 14, -2), ("pe_w2", 0, -1), ("gp_kv", 15, -2), ("dv_prod", 11, -2), ("dv_scan", 14, -2),
    ("pe_red", 2, -2), ("act_k", 0, -1), ("dv_scan", 15, -2), ("pe_mus", 4, -1), ("dv_prod", 12, -2), ("dv_prod", 13, -2),
    ("dv_prod", 14, -2), ("gp_add", 2, -1), ("dv_prod", 15, -2), ("act_ew", 0, -1), ("dv_ob", 0, -2), ("gp_gather", 0, 1),
    ("pe_red", 3, -2), ("dv_mus", 8, -1), ("pe_mus", 3, -1), ("act_d", 0, -1), ("dv_ob", 1, -2), ("pe_pv", 0, -1),
    ("dv_signs", 0, -1), ("dv_mus", 6, -1), ("sp_idx", 0, 3), ("dv_mus", 7, -1), ("dv_mus", 9, -1), ("act_sq", 0, -2),
    ("gp_sq", 0, -2), ("pe_var", 0, -2), ("pe_agT", 0, 1), ("act_sdo", 0, -2), ("gp_add", 3, -1), ("act_agT", 0, 1),
    ("gp_add", 4, -1), ("dv_idx", 0, 3), ("pe_pv", 1, -1), ("act_v", 0, -1), ("act_v", 1, -1), ("pe_lora", 0, 1),
    ("pe_proj", 4, -1), ("dv_on", 0, -2), ("gp_delta", 0, 0), ("act_y", 0, -2), ("gp_gate", 0, -2), ("dv_lora", 0, 1),
    ("sp_spread", 0, -1), ("dv_lora", 1, 1), ("sp_spread", 1, -1), ("dv_mix0", 0, 0), ("dv_st1", 0, 1), ("sp_spread", 2, -1),
    ("act_sd1", 0, 1), ("gp_kv", 0, -1), ("dv_ruk", 0, -1), ("sp_spread", 3, -1), ("sp_spread", 4, -1), ("sp_spread", 5, -1),
    ("dv_scan", 0, -1), ("sp_spread", 6, -1), ("dv_r1", 0, 1), ("dv_prod", 0, -1), ("gp_kv", 1, -1), ("gp_kv", 2, -1),
    ("dv_scan", 1, -1), ("pe_z", 0, 0), ("gp_kv", 3, -1), ("dv_prod", 1, -1), ("sp_spread", 7, -1), ("pe_wo", 0, -2),
    ("gp_kv", 4, -1), ("pe_wo", 1, -2), ("sp_spread", 8, -1), ("gp_kv", 5, -1), ("dv_scan", 2, -1), ("dv_scan", 3, -1),
    ("dv_prod", 2, -1), ("gp_kv", 6, -1), ("dv_scan", 4, -1), ("dv_prod", 3, -1), ("act_n1", 0, 1), ("dv_scan", 5, -1),
    ("act_z", 0, 0), ("dv_zl", 0, 0), ("pe_bs", 0, -1), ("pe_xT", 0, 1), ("dv_h2", 0, -2), ("dv_h2", 1, -2),
    ("dv_prod", 4, -1), ("pe_xT", 1, 1), ("act_xT", 0, 1), ("dv_st2", 0, -2), ("act_bs", 0, -1), ("dv_prod", 5, -1),
    ("sp_spread", 9, -1), ("pe_pg", 0, -1), ("pe_zr", 0, 0), ("gp_kv", 7, -1), ("sp_spread", 10, -1), ("dv_scan", 6, -1),
    ("gp_kv", 8, -1), ("act_xT", 1, 1), ("dv_scan", 7, -1), ("act_sd2", 0, -2), ("pe_pg", 1, -1), ("dv_r2", 0, -2),
    ("dv_scan", 8, -1), ("dv_prod", 6, -1), ("gp_kv", 9, -1), ("gp_bonus", 0, -1), ("dv_prod", 7, -1), ("act_th", 0, -1),
    ("act_n2", 0, -2), ("dv_gate", 0, -1), ("dv_scan", 9, -1), ("pe_yT", 0, -2), ("pe_zr", 1, 0), ("gp_kv", 10, -1),
    ("act_zr", 0, 0), ("pe_yT", 1, -2), ("dv_prod", 8, -1), ("sp_spread", 11, -1), ("gp_kv", 11, -1), ("act_th", 1, -1),
]
FILLS = {
    ("pe_agT", 0): ["agT"], ("pe_lora", 0): ["lora0", "lora1"],
    ("pe_xT", 0): ["xT0"], ("pe_xT", 1): ["xT1"], ("pe_z", 0): ["z"],
    ("pe_zr", 0): ["zr0"], ("pe_zr", 1): ["zr1"], ("pe_mus", 0): ["mu0a", "mu0b"], ("pe_mus", 1): ["mu1a", "mu1b"],
    ("pe_mus", 2): ["mu2a", "mu2b"], ("pe_mus", 3): ["mu3a", "mu3b"], ("pe_mus", 4): ["mu4a", "mu4b"],
    ("pe_proj", 0): ["pw"], ("pe_proj", 1): ["pk"], ("pe_pv", 0): ["pv0"], ("pe_pv", 1): ["pv1"],
    ("pe_pg", 0): ["pg0"], ("pe_pg", 1): ["pg1"], ("pe_w2", 0): ["w2"], ("pe_bs", 0): ["bs"],
    ("pe_var", 0): ["var"], ("pe_wo", 0): ["wo0"], ("pe_wo", 1): ["wo1"],
    ("pe_yT", 0): ["yT0"], ("pe_yT", 1): ["yT1"], ("pe_ffn", 0): ["f0"], ("pe_ffn", 1): ["f1"],
    ("pe_fT", 0): ["fT0"], ("pe_fT", 1): ["fT1"],
}


MOST, LEAST = max(x[2] for x in SCHEDULE), min(x[2] for x in SCHEDULE)
FIRST_LOOPED = 1 - LEAST


def fill_places():
    bank, per = {}, [0] * NW
    order = [(n, stage) for what, a, stage in SCHEDULE for n in FILLS.get((what, a), [])]
    for i, (n, stage) in enumerate(order):
        bank[n] = i % NW
        per[i % NW] += 1
    count, seen = {n: {} for n, _ in order}, [0] * NW
    for s in range(-MOST, NBLK - LEAST):
        for n, stage in order:
            if 0 <= s + stage < NBLK:
                seen[bank[n]] += 1
                count[n][s + stage] = seen[bank[n]]
    return bank, count, per


BANK, COUNT, PER = fill_places()
POS = {x[:2]: (i, x[2]) for i, x in enumerate(SCHEDULE)}
Y_TURNED_BEFORE = POS["act_n2", 0][1] - POS["act_n1", 0][1] - (POS["act_n2", 0][0] > POS["act_n1", 0][0])
X_TURNED_BEFORE = POS["act_n1", 0][1] - POS["act_n2", 0][1] - (POS["act_n1", 0][0] > POS["act_n2", 0][0])


class Block:

    def __init__(self, off, turn=None):
        self.off, self.turn = off, turn

    def __add__(self, n):
        return Block(self.off + n, self.turn)

    def times(self, per, c=0):
        const = per * self.off + c
        if self.turn is None:
            return const
        assert const > 0
        return self.turn * (per * LOOPED) + const

    def round(self, n, per, c=0):
        const = per * (self.off // n) + c
        if self.turn is None:
            return const
        assert const > 0
        return self.turn * (per * (LOOPED // n)) + const

    def fill(self, name, c=0):
        const = COUNT[name][self.off] + c
        if self.turn is None:
            return const
        per = PER[BANK[name]] * LOOPED
        assert const > 0 and COUNT[name][self.off + LOOPED] + c - const == per
        return self.turn * per + const


def wait(eng, sem, value):
    if isinstance(value, int) and value <= 0:
        return
    eng.wait_ge(sem, value)


def whole_run(eng, pieces):
    def step(off, turn=None):
        for what, a, stage in SCHEDULE:
            b = off + stage
            if what in pieces and (turn is not None or 0 <= b < NBLK):
                pieces[what](Block(b, turn), a)

    turns = (NBLK - MOST - FIRST_LOOPED) // LOOPED
    for s in range(-MOST, FIRST_LOOPED):
        step(s)
    with eng.Fori(0, turns) as turn:
        for u in range(LOOPED):
            step(FIRST_LOOPED + u, turn)
    for s in range(FIRST_LOOPED + turns * LOOPED, NBLK - LEAST):
        step(s)


def tower_kernel(nc, x, w_tok, a_tok, b_tok, vecs, wx1, wx2, wr, ww1, ww2, wk, wv, wg, wo, w_ffn, out):
    ctx = ExitStack()
    with ctx:
        def sb(name, shape, dt=F32):
            return ctx.enter_context(nc.sbuf_tensor(name, shape, dt))

        def pb(name):
            return ctx.enter_context(nc.psum_tensor(name, [P, 512], F32))

        def sem(name):
            return ctx.enter_context(nc.semaphore(name))

        wx1_s = sb("wx1_s", [P, KD, 5 * RLO])
        wx2_s = sb("wx2_s", [P, 5, D], F32R)
        wr_s = sb("wr_s", [P, KD, NH * HK])
        ww1_s = sb("ww1_s", [P, KD, GLO])
        ww2_s = sb("ww2_s", [GLO, NH * HK])
        wk_s = sb("wk_s", [P, KD, NH * HK])
        wv_s = sb("wv_s", [P, KD, D])
        wg_s = sb("wg_s", [P, KD, D])
        wo_s = sb("wo_s", [P, VT, D])
        wf_s = sb("wf_s", [P, KD, D], F32R)
        bt_s = sb("bt_s", [P // TC + RANK, D])
        vec_s = sb("vec_s", [P, 20])
        ident = sb("ident", [P, P])
        rank_sel = sb("rank_sel", [P, 18, RLO], F32R)
        low_z = sb("low_z", [P, 1])
        low_w = sb("low_w", [P, 1])
        head_sel = sb("head_sel", [P, HH, VG, NH])
        head_mean = sb("head_mean", [P, VG, NH])
        eps_s = sb("eps_s", [P, 1])
        gn_half = sb("gn_half", [P, 2 * VT])
        alpha = sb("alpha", [P, KD])
        pool_cell = sb("pool_cell", [1, 32])
        dve_cell = sb("dve_cell", [1, 32])
        idx_i = sb("idx_i", [P, 4, TC], I32)
        idx_f = sb("idx_f", [P, 2, TC])
        idx_u = sb("idx_u", [P, 4, TC], U32)
        h = sb("h", [P, 4, TC, D])
        ag = sb("ag", [P, 2, TC, P // TC])
        agT = sb("agT_s", [P, P])
        stats = sb("stats", [P, 2, TC, 6])
        mv = sb("mv", [P, 2, TC, 2])
        sd = sb("sd", [P, 2, TC])
        rs = sb("rs", [P, 2, TC])
        shift = sb("shift", [P, 2, TC])
        xn = sb("xn", [P, TC, D])
        yn = xn
        xT = sb("xT", [P, 2, KD, TB + 1])
        delta = sb("delta", [P, KD, TB])
        mx = sb("mx", [P, MXRING, KD, TB])
        z0_high = sb("z0_high", [P, TB], F32R)
        z0_low = sb("z0_low", [P, TB], F32R)
        z0 = sb("z0", [P, TB])
        z1 = sb("z1", [P, TB])
        zs = sb("zs", [P, 5, TB], F32R)
        t2 = sb("t2", [GLO, TB])
        ew = sb("ew", [P, HH, TB])
        kT = sb("kT", [P, 2, HH, TB])
        vT = sb("vT", [P, 2, VT, TB])
        gate = sb("gate", [P, 2, VT, TB])
        ruk = sb("ruk", [P, HH, TB])
        bsb = sb("bsb", [P, TB])
        vB = sb("vB", [P, VRING, HH, TB])
        kv = sb("kv", [P, KVRING, HH, TB])
        state_flat = sb("state", [P, HV * HH * (TB + 1)])
        state = state_flat[:, :].rearrange("p (v a t) -> p v a t", v=HV, a=HH)
        wv_mean = state_flat[:, 2 * KD * D:2 * KD * D + KD * NH].rearrange("p (k v h) -> p k v h", k=KD, v=1)
        wx2_in = state_flat[:, 2 * KD * D + KD * NH:(2 * KD + 5) * D + KD * NH].rearrange("p (m n) -> p m n", m=5)
        zeros = state_flat[:, 7 * KD * D // 2:7 * KD * D // 2 + 18 * RLO].rearrange("p (q r) -> p q r", q=18)
        wf = state_flat[:, 0:KD * D].rearrange("p (k n) -> p k n", k=KD)
        bw = state_flat[:, KD * D:2 * KD * D].rearrange("p (k n) -> p k n", k=KD)
        ob = sb("ob", [P, 2, VT, TB])
        sdo = sb("sdo", [P, TB])
        yT = sb("yT", [P, VT, TB])
        sq, fT = yT[:, :, :], yT[:, :, :]
        y2T_high = sb("y2T_high", [P, KD, TC, P], F32R)
        y2T_low = sb("y2T_low", [P, KD, TC, P], F32R)

        W = [pb(f"W{i}") for i in range(NW)]
        R = pb("R")
        DK = pb("DK")
        O = [pb("O0"), pb("O1")]
        r_t = R[:, :].rearrange("p (a t) -> p a t", a=HH)
        d_t = DK[:, :].rearrange("p (a t) -> p a t", a=HH)

        w_first = sem("first_weights_loaded")
        w_x = sem("shift_weights_loaded")
        w_v = sem("value_weight_loaded")
        w_f = sem("ffn_weight_loaded")
        w_in = sem("weights_loaded")
        c_gn = sem("norm_weights_halved")
        c_k = sem("constants_ready")
        c_cell = [sem("pool_cell_set"), sem("dve_cell_set")]
        c_sel = sem("selection_steps")
        c_low = sem("low_rows_marked")
        c_w = sem("shift_weight_split")
        c_rank = sem("rank_selection_set")
        c_v = sem("value_weight_centred")
        c_f = sem("ffn_weight_steps")
        c_ft = sem("ffn_weight_turned")
        c_fc = sem("ffn_weight_copied")
        full = [sem(f"bank{i}_full") for i in range(NW)]
        free = [sem(f"bank{i}_emptied") for i in range(NW)]
        idx_in = [sem(f"idx_in{i}") for i in range(4)]
        idx_st = sem("idx_steps")
        rows_in = [sem(f"rows_in{i}") for i in range(4)]
        stored = [sem(f"stored{i}") for i in range(4)]
        v_h = sem("h_summed")
        v_st = sem("stats_done")
        v_mv = sem("mean_var_done")
        a_sd = sem("std_done")
        v_rs = sem("rstd_done")
        a_xn = sem("x_normed")
        a_yh = sem("y_high_parts")
        p_col = sem("shift_column_set")
        p_delta = sem("delta_done")
        v_mx0 = sem("mix0_done")
        v_zl = sem("z_split")
        p_add = sem("mixed")
        a_th = sem("gate_tanh_done")
        a_d = sem("decay_set")
        pe_r = sem("r_ready")
        v_ruk = sem("ruk_done")
        p_bv = sem("bonus_done")
        vb_in = [sem(f"v_spread{i}") for i in range(VRING)]
        p_kv = sem("kv_done")
        v_c = sem("state_column_set")
        v_scan = sem("scanned")
        v_p = sem("products_done")
        pe_red = sem("heads_reduced")
        v_ob = sem("o_summed")
        a_sq = sem("o_squared")
        p_sq = sem("squares_added")
        v_rg = sem("o_rstd_done")
        v_on = sem("o_normed")
        a_y = sem("o_scaled")
        p_y = sem("o_gated")
        v_h2 = sem("h_attn_summed")
        v_st2 = sem("stats2_done")
        v_mv2 = sem("mean_var2_done")
        a_sd2 = sem("std2_done")
        v_rs2 = sem("rstd2_done")
        a_yn = sem("y_normed")
        a_f = sem("ffn_scaled")

        block = ctx.enter_context(nc.Block())

        def emptied(eng, b, name):
            wait(eng, free[BANK[name]], b.fill(name))

        def first(b):
            return b.turn is None and b.off == 0

        def filled(eng, b, name):
            wait(eng, full[BANK[name]], b.fill(name))
            return W[BANK[name]]

        def take_wait(ops, cells, taken):
            taken.append(len(taken) + 1)
            ops.tensor_tensor(cells[:, taken[-1]:taken[-1] + 1], cells[:, 0:1], cells[:, 0:1], ALU.add)

        @block.sync
        def _(sp):
            for dst, src in ((vec_s[:, :], vecs), (bt_s[0:RANK, :], b_tok), (bt_s[P // TC:P // TC + RANK, :], b_tok)):
                sp.dma_start(dst, src).then_inc(w_first, 16)

            def load_idx(b, _):
                q = b.off % 4
                src = x[bass.ds(sp.snap(b.times(1)), 1), :, :].rearrange("b p c -> (b p) c") if b.turn is not None else x[b.off, :, :]
                wait(sp, idx_st, b.times(3, 3 - 12))
                sp.dma_start(idx_i[:, q, :], src).then_inc(idx_in[q], 16)

            def spread(b, v):
                if v == 0:
                    emptied(sp, b, "pv1")
                else:
                    wait(sp, p_kv, b.times(HV, v + 2 - VRING))
                for hh in range(HH):
                    r0 = NH * (v % VG) + NH // HH * hh
                    sp.dma_start(vB[:, v % VRING, hh, :],
                                 vT[r0:r0 + NH // HH, b.off % 2, v // VG:v // VG + 1, :].to_broadcast([NH // HH, HK, TB]))\
                        .then_inc(vb_in[v % VRING], 16)

            whole_run(sp, {"sp_idx": load_idx, "sp_spread": spread})

        @block.gpsimd
        def _(pool):
            pool_taken = []
            nc.gpsimd.memset(pool_cell[:, :], 0.0).then_inc(c_cell[0], 1)
            pool.wait_ge(c_cell[0], 1)
            nc.gpsimd.memset(ident[:, :], 0.0).then_inc(c_sel, 1)
            nc.gpsimd.memset(head_sel[:, :, :, :], 1.0).then_inc(c_sel, 1)
            nc.gpsimd.memset(head_mean[:, :, :], 0.0).then_inc(c_sel, 1)
            nc.gpsimd.memset(eps_s[:, :], EPS).then_inc(c_sel, 1)
            nc.gpsimd.memset(ag[:, :, :, :], 0.0).then_inc(c_sel, 1)
            nc.gpsimd.memset(zeros, 0.0).then_inc(c_sel, 1)
            count = 6
            pool.wait_ge(c_sel, count)
            nc.gpsimd.affine_select(out=ident[:, :], in_=ident[:, :], compare_op=ALU.not_equal, fill=1.0, base=0,
                                    pattern=[[-1, P]], channel_multiplier=1).then_inc(c_k, 1)
            for hh in range(HH):
                nc.gpsimd.affine_select(out=head_sel[:, hh, :, :], in_=head_sel[:, hh, :, :], compare_op=ALU.is_ge, fill=0.0,
                                        base=HK * NH // HH * hh, pattern=[[0, VG], [-HK, NH]], channel_multiplier=1).then_inc(c_sel, 1)
                count += 1
                pool.wait_ge(c_sel, count)
                nc.gpsimd.affine_select(out=head_sel[:, hh, :, :], in_=head_sel[:, hh, :, :], compare_op=ALU.is_ge, fill=0.0,
                                        base=HK - 1 - HK * NH // HH * hh, pattern=[[0, VG], [HK, NH]], channel_multiplier=-1).then_inc(c_k, 1)
            for vi in range(VG):
                ins = nc.gpsimd.affine_select(out=head_mean[:, :, :], in_=head_mean[:, :, :], compare_op=ALU.not_equal, fill=1.0 / HV,
                                              base=-NH * vi, pattern=[[0, VG], [-1, NH]], channel_multiplier=1)
                if vi < VG - 1:
                    ins.then_inc(c_sel, 1)
                    count += 1
                    pool.wait_ge(c_sel, count)
                else:
                    ins.then_inc(c_k, 1)

            def gather(b, _):
                q = b.off % 4
                wait(pool, stored[q], b.round(4, 16))
                if b.off >= 2:
                    emptied(pool, b + -2, "agT")
                wait(pool, idx_st, b.times(3, 3))
                take_wait(nc.gpsimd, pool_cell, pool_taken)
                for c in range(TC):
                    nc.gpsimd.indirect_dma_start(h[:, q, c, :], None, w_tok, bass.IndirectOffsetOnAxis(ap=idx_u[:, q, c:c + 1], axis=0))\
                        .then_inc(rows_in[q], 16)
                    nc.gpsimd.indirect_dma_start(ag[:, q % 2, c, 0:RANK], None, a_tok, bass.IndirectOffsetOnAxis(ap=idx_u[:, q, c:c + 1], axis=0))\
                        .then_inc(rows_in[q], 16)

            def shift_difference(n, _):
                q = n.off % 2
                emptied(pool, n, "xT1")
                take_wait(nc.gpsimd, pool_cell, pool_taken)
                if n.off % PER_SEQ == 0:
                    nc.gpsimd.memset(xT[:, q, :, 0:1], 0.0).then_inc(p_col, 1)
                else:
                    nc.gpsimd.tensor_copy(xT[:, q, :, 0:1], xT[:, 1 - q, :, TB:TB + 1]).then_inc(p_col, 1)
                if n.off > 0:
                    emptied(pool, n + -1, "mu4b")
                pool.wait_ge(p_col, n.times(1, 1))
                nc.gpsimd.tensor_tensor(delta[:, :, :], xT[:, q, :, 0:TB], xT[:, q, :, 1:TB + 1], ALU.subtract).then_inc(p_delta, 1)

            def mix_add(n, a):
                emptied(pool, n, f"mu{a}b")
                m = mx[:, (1 + a) % MXRING, :, :]
                nc.gpsimd.tensor_tensor(m, m, xT[:, n.off % 2, :, 1:TB + 1], ALU.add).then_inc(p_add, 1)

            def key_value(j, v):
                if v == 0:
                    emptied(pool, j, "pk")
                if v % 2 == 0:
                    wait(pool, v_scan, j.times(HV, v + 2 - KVRING))
                wait(pool, vb_in[v % VRING], j.times(32 * HV // VRING, 32 * (v // VRING + 1)))
                nc.gpsimd.tensor_tensor(kv[:, v % KVRING, :, :], vB[:, v % VRING, :, :], kT[:, j.off % 2, :, :], ALU.mult)\
                    .then_inc(p_kv, 1)

            def bonus(j, _):
                emptied(pool, j, "pv1")
                wait(pool, a_y, j.times(1, -1))
                emptied(pool, j, "bs")
                nc.gpsimd.tensor_tensor(ob[:, j.off % 2, :, :], vT[:, j.off % 2, :, :],
                                        bsb[:, :].rearrange("p (m t) -> p m t", m=1).to_broadcast([P, VT, TB]), ALU.mult)\
                    .then_inc(p_bv, 1)

            def add_squares(t, _):
                pool.wait_ge(a_sq, t.times(1, 1))
                nc.gpsimd.tensor_tensor(sq[:, 0:2, :], sq[:, 0:2, :], sq[:, 2:4, :], ALU.add).then_inc(p_sq, 1)
                pool.wait_ge(p_sq, t.times(2, 1))
                nc.gpsimd.tensor_tensor(sq[:, 0, :], sq[:, 0, :], sq[:, 1, :], ALU.add).then_inc(p_sq, 1)

            def gated(t, _):
                wait(pool, a_y, t.times(1, 1))
                nc.gpsimd.tensor_tensor(yT[:, :, :], yT[:, :, :], gate[:, t.off % 2, :, :], ALU.mult).then_inc(p_y, 1)

            whole_run(pool, {"gp_gather": gather, "gp_delta": shift_difference, "gp_add": mix_add, "gp_kv": key_value,
                             "gp_bonus": bonus, "gp_sq": add_squares, "gp_gate": gated})

        @block.scalar
        def _(act):
            act.dma_start(wx1_s[:, :, :], wx1.rearrange("(k p) n -> p k n", p=P)).then_inc(w_x, 16)
            for q in range(P // RLO):
                act.dma_start(wx2_in[q * RLO:(q + 1) * RLO, :, :], wx2.rearrange("(m r) n -> r m n", m=5)).then_inc(w_x, 16)
            act.wait_ge(w_first, 16 * 3)
            act.wait_ge(c_sel, 6)
            nc.scalar.mul(gn_half[:, :], vec_s[:, NC_GW:NC_GW + 2 * VT], 0.5).then_inc(c_gn, 1)
            act.wait_ge(c_gn, 1)

            def split_shift_weight():
                act.wait_ge(w_x, 16 * (1 + P // RLO))
                nc.scalar.activation(wx2_s[:, :, :], wx2_in, ACT.Copy).then_inc(c_w, 1)
                act.wait_ge(c_k, 1)
                nc.scalar.activation(rank_sel[:, :, :], zeros, ACT.Copy).then_inc(c_rank, 1)
                act.wait_ge(c_rank, 1)
                for m in range(4):
                    ins = nc.scalar.activation(rank_sel[:, 2 + 4 * m:4 + 4 * m, :], ident[:, m * RLO:(m + 1) * RLO].rearrange("p (q r) -> p q r", q=1)
                                               .to_broadcast([P, 2, RLO]), ACT.Copy)
                ins.then_inc(c_rank, 1)

            act.wait_ge(rows_in[0], 64)
            act.dma_start(ww1_s[:, :, :], ww1.rearrange("(k p) n -> p k n", p=P)).then_inc(w_in, 16)
            act.dma_start(wk_s[:, :, :], wk.rearrange("(k p) n -> p k n", p=P)).then_inc(w_in, 16)
            act.dma_start(wv_s[:, :, :], wv.rearrange("(k p) n -> p k n", p=P)).then_inc(w_v, 16)
            act.dma_start(wf, w_ffn.rearrange("(k p) n -> p k n", p=P)).then_inc(w_f, 16)
            act.dma_start(ww2_s[:, :], ww2).then_inc(w_in, 16)
            act.dma_start(wg_s[:, :, :], wg.rearrange("(k p) n -> p k n", p=P)).then_inc(w_in, 16)
            act.dma_start(wr_s[:, :, :], wr.rearrange("(k p) n -> p k n", p=P)).then_inc(w_in, 16)
            act.dma_start(wo_s[:, :, :], wo.rearrange("(k p) n -> p k n", p=P)).then_inc(w_in, 16)
            split_shift_weight()

            def take(b, name, dst, src, func=ACT.Copy, last=True, **more):
                w = filled(act, b, name)
                ins = nc.scalar.activation(dst, src(w), func, **more)
                if last:
                    ins.then_inc(free[BANK[name]], 1)

            def lora_rows(n, _):
                take(n, "agT", agT[:, :], lambda w: w[:, 0:P])

            def deviation1(n, _):
                wait(act, v_mv, n.times(1, 1))
                nc.scalar.activation(sd[:, 0, :], mv[:, 0, :, 1], ACT.Sqrt, bias=eps_s[:, 0:1]).then_inc(a_sd, 1)

            def deviation2(t, _):
                wait(act, v_mv2, t.times(1, 1))
                nc.scalar.activation(sd[:, 1, :], mv[:, 1, :, 1], ACT.Sqrt, bias=eps_s[:, 0:1]).then_inc(a_sd2, 1)

            def layer_norm(b, k, rs_sem, done):
                q = b.off % 4
                act.wait_ge(rs_sem, b.times(2, 2))
                for c in range(TC):
                    ins = nc.scalar.activation(xn[:, c, :], h[:, q, c, :], ACT.Identity, scale=rs[:, k, c:c + 1], bias=shift[:, k, c:c + 1])
                ins.then_inc(done, 1)

            def norm1(n, _):
                if n.off + Y_TURNED_BEFORE >= 0:
                    filled(act, n + Y_TURNED_BEFORE, "yT1")
                layer_norm(n, 0, v_rs, a_xn)

            def norm2(t, _):
                if t.off + X_TURNED_BEFORE < NBLK:
                    filled(act, t + X_TURNED_BEFORE, "xT1")
                layer_norm(t, 1, v_rs2, a_yn)

            def x_turned(n, i):
                if i == 0:
                    wait(act, p_add, n.times(5, -5))
                    wait(act, p_col, n.times(1))
                take(n, f"xT{i}", xT[:, n.off % 2, 2 * i:2 * i + 2, 1:TB + 1].rearrange("p f (t c) -> p f t c", c=TC),
                     lambda w: w[:, :].rearrange("p (f c t) -> p f t c", f=2, c=TC))

            def z_tanh(n, _):
                take(n, "z", z0[:, :], lambda w: w[:, 0:TB], ACT.Tanh, last=False)
                take(n, "z", z0_high[:, :], lambda w: w[:, 0:TB], ACT.Tanh, last=False)
                take(n, "z", z1[:, :], lambda w: w[:, TB:2 * TB], ACT.Tanh, last=False)
                take(n, "z", zs[:, MIX_G, :], lambda w: w[:, TB:2 * TB], ACT.Tanh)

            def z_rows(n, i):
                take(n, f"zr{i}", zs[:, 2 * i:2 * i + 2, :], lambda w: w[:, :].rearrange("p (m t) -> p m t", m=2))

            def decay_tanh(n, _):
                take(n, "pw", t2[:, :], lambda w: w[0:GLO, 0:TB], ACT.Tanh)

            def decay_exp(n, _):
                w = filled(act, n, "w2")
                for hh in range(HH):
                    ins = nc.scalar.activation(ew[:, hh, :], w[:, hh * TB:hh * TB + TB], ACT.Exp,
                                               bias=vec_s[:, NC_BW + hh:NC_BW + hh + 1])
                ins.then_inc(free[BANK["w2"]], 1)

            def decay(n, _):
                emptied(act, n, "w2")
                wait(act, v_scan, n.times(HV))
                nc.scalar.activation(DK[:, :], ew[:, :, :].rearrange("p a t -> p (a t)"), ACT.Exp, scale=-1.0).then_inc(a_d, 1)

            def k_out(n, _):
                wait(act, p_kv, n.times(HV, -HV))
                wait(act, v_ruk, n.times(1, -1))
                take(n, "pk", kT[:, n.off % 2, :, :], lambda w: w[:, :].rearrange("p (a t) -> p a t", a=HH))

            def v_out(n, i):
                if i == 0:
                    wait(act, p_kv, n.times(HV, -HV))
                    wait(act, p_bv, n.times(1, -1))
                take(n, f"pv{i}", vT[:, n.off % 2, 2 * i:2 * i + 2, :], lambda w: w[:, :].rearrange("p (m t) -> p m t", m=2))

            def gate_tanh(n, i):
                if i == 0:
                    wait(act, p_y, n.times(1, -1))
                w = filled(act, n, f"pg{i}")
                nc.scalar.activation(gate[:, n.off % 2, 2 * i:2 * i + 2, :], w[:, :].rearrange("p (m t) -> p m t", m=2),
                                     ACT.Tanh, scale=0.5).then_inc(a_th, 1)

            def bonus_sums(j, _):
                wait(act, p_bv, j.times(1))
                take(j, "bs", bsb[:, :], lambda w: w[:, 0:TB])

            def squares(t, _):
                wait(act, v_ob, t.times(2, 2))
                if t.off > 0:
                    filled(act, t + -1, "fT1")
                nc.scalar.activation(sq, ob[:, t.off % 2, :, :], ACT.Square).then_inc(a_sq, 1)

            def deviation_o(t, _):
                wait(act, v_on, t.times(1))
                take(t, "var", sdo[:, :], lambda w: w[:, 0:TB], ACT.Sqrt, bias=eps_s[:, 0:1])

            def scaled(t, _):
                wait(act, v_on, t.times(1, 1))
                for m in range(VT):
                    ins = nc.scalar.activation(yT[:, m, :], ob[:, t.off % 2, m, :], ACT.Identity,
                                               bias=gn_half[:, VT + m:VT + m + 1], scale=gn_half[:, m:m + 1])
                ins.then_inc(a_y, 1)

            def y_turned(t, i):
                w = filled(act, t, f"yT{i}")
                nc.scalar.activation(y2T_high[:, 2 * i:2 * i + 2, :, :], w[:, :].rearrange("p (f c t) -> p f c t", f=2, c=TC), ACT.Copy)\
                    .then_inc(a_yh, 1)

            def ffn_out(t, i):
                w = filled(act, t, f"f{i}")
                for g in range(2):
                    o = 2 * i + g
                    ins = nc.scalar.activation(fT[:, o, :], w[:, g * TB:g * TB + TB], ACT.Identity, scale=alpha[:, o:o + 1],
                                               bias=vec_s[:, NC_FB + o:NC_FB + o + 1])
                ins.then_inc(free[BANK[f"f{i}"]], 1)

            def store(t, _):
                at = bass.ds(t.times(1), 1) if t.turn is not None else slice(t.off, t.off + 1)
                emptied(act, t, "fT1")
                act.dma_start(out[at, :, :].rearrange("b p n -> (b p) n"), h[:, t.off % 4, :, :].rearrange("p c d -> p (c d)"))\
                    .then_inc(stored[t.off % 4], 16)

            whole_run(act, {"act_agT": lora_rows, "act_sd1": deviation1, "act_sd2": deviation2, "act_xT": x_turned, "act_z": z_tanh, "act_zr": z_rows,
                            "act_t2": decay_tanh, "act_ew": decay_exp, "act_d": decay, "act_k": k_out, "act_v": v_out,
                            "act_th": gate_tanh, "act_bs": bonus_sums, "act_sq": squares, "act_sdo": deviation_o,
                            "act_y": scaled, "act_f": ffn_out, "act_n1": norm1, "act_n2": norm2, "act_yT": y_turned, "act_store": store})
            for q in range(4):
                act.wait_ge(stored[q], 16 * (NBLK // 4))

        @block.vector
        def _(dve):
            dve_taken = []
            nc.vector.memset(dve_cell[:, :], 0.0).then_inc(c_cell[1], 1)
            dve.wait_ge(c_cell[1], 1)
            for q in range(P // RLO):
                nc.vector.memset(low_z[q * RLO:(q + 1) * RLO, :], -1.0 if q >= 2 else 0.0).then_inc(c_low, 1)
                nc.vector.memset(low_w[q * RLO:(q + 1) * RLO, :], -1.0 if q % 2 == 1 else 0.0).then_inc(c_low, 1)
            dve.wait_ge(c_low, 2 * P // RLO)

            def low_shift_weight():
                dve.wait_ge(c_w, 1)
                nc.vector.scalar_tensor_tensor(wx2_s[:, :, :], wx2_s[:, :, :].bitcast(F32), low_w[:, 0:1], wx2_in, ALU.mult, ALU.add)\
                    .then_inc(c_w, 1)

            def centre_value_weight():
                dve.wait_ge(w_v, 16)
                nc.vector.tensor_reduce(wv_mean[:, :, 0, :], wv_s[:, :, :].rearrange("p k (v h) -> p k h v", v=HV), AX.X, ALU.add).then_inc(c_v, 1)
                dve.wait_ge(c_v, 1)
                for k in range(KD):
                    wv_k = wv_s[:, k, :].rearrange("p (v h) -> p v h", v=HV)
                    nc.vector.scalar_tensor_tensor(wv_k, wv_mean[:, k, :, :].to_broadcast([P, HV, NH]), -1.0 / HV, wv_k,
                                                   ALU.mult, ALU.add).then_inc(c_v, 1)

            def binarise():
                dve.wait_ge(w_f, 16)
                nc.vector.tensor_reduce(alpha[:, :], wf, AX.X, ALU.add, apply_absolute_value=True).then_inc(c_f, 1)
                dve.wait_ge(c_f, 1)
                nc.vector.tensor_scalar(alpha[:, :], alpha[:, :], 1.0 / D, None, ALU.mult).then_inc(c_f, 1)
                nc.vector.tensor_scalar(bw, wf, 0.0, 2.0, ALU.is_ge, ALU.mult).then_inc(c_f, 1)

            def take_signs(n, _):
                if not first(n):
                    return
                for f in range(KD):
                    dve.wait_ge(c_ft, f + 1)
                    nc.vector.tensor_scalar(wf_s[:, f, :], O[f % 2][:, :], -1.0, None, ALU.add).then_inc(c_fc, 1)
                dve.wait_ge(c_rank, 2)
                dve.wait_ge(c_fc, KD)

            def layer_stats(b, k, stats_sem, mv_sem, done):
                q = b.off % 4
                wait(dve, done, b.times(1))
                for c in range(TC):
                    ins = nc.vector.bn_stats(stats[:, k, c, :], h[:, q, c, :])
                ins.then_inc(stats_sem, 1)
                dve.wait_ge(stats_sem, b.times(1, 1))
                take_wait(nc.vector, dve_cell, dve_taken)
                for c in range(TC):
                    ins = nc.vector.bn_aggr(mv[:, k, c, :], stats[:, k, c, :])
                ins.then_inc(mv_sem, 1)

            def scale_and_shift(b, k, sd_sem, rs_sem):
                dve.wait_ge(sd_sem, b.times(1, 1))
                nc.vector.reciprocal(rs[:, k, :], sd[:, k, :]).then_inc(rs_sem, 1)
                dve.wait_ge(rs_sem, b.times(2, 1))
                nc.vector.scalar_tensor_tensor(shift[:, k, :], mv[:, k, :, 0], -1.0, rs[:, k, :], ALU.mult, ALU.mult).then_inc(rs_sem, 1)

            def clamp_idx(b, _):
                q = b.off % 4
                wait(dve, idx_in[q], b.round(4, 16, 16))
                wait(dve, idx_st, b.times(3))
                wait(dve, rows_in[q], b.round(4, 64))
                nc.vector.tensor_scalar(idx_f[:, 0, :], idx_i[:, q, :], float(VOCAB - 1), float(-VOCAB), ALU.min, ALU.max).then_inc(idx_st, 1)
                dve.wait_ge(idx_st, b.times(3, 1))
                nc.vector.tensor_scalar(idx_f[:, 1, :], idx_f[:, 0, :], 0.0, float(VOCAB), ALU.is_lt, ALU.mult).then_inc(idx_st, 1)
                dve.wait_ge(idx_st, b.times(3, 2))
                nc.vector.tensor_tensor(idx_u[:, q, :], idx_f[:, 0, :], idx_f[:, 1, :], ALU.add).then_inc(idx_st, 1)

            def add_fill(b, name, c):
                w = filled(dve, b, name)
                hc = h[:, b.off % 4, c, :]
                nc.vector.tensor_tensor(hc, hc, w[:, :], ALU.add).then_inc(free[BANK[name]], 1)

            def add_lora(n, c):
                if first(n) and c == 0:
                    low_shift_weight()
                add_fill(n, f"lora{c}", c)

            def add_attention(t, c):
                add_fill(t, f"wo{c}", c)

            def add_ffn(t, c):
                add_fill(t, f"fT{c}", c)

            def stats1(n, _):
                emptied(dve, n, "lora1")
                layer_stats(n, 0, v_st, v_mv, a_xn)

            def stats2(t, _):
                emptied(dve, t, "wo1")
                layer_stats(t, 1, v_st2, v_mv2, a_yn)

            def scale1(n, _):
                scale_and_shift(n, 0, a_sd, v_rs)

            def scale2(t, _):
                scale_and_shift(t, 1, a_sd2, v_rs2)

            def split_y(t, i):
                dve.wait_ge(a_yh, t.times(2, i + 1))
                w = filled(dve, t, f"yT{i}")
                nc.vector.tensor_tensor(y2T_low[:, 2 * i:2 * i + 2, :, :], w[:, :].rearrange("p (f c t) -> p f c t", f=2, c=TC),
                                        y2T_high[:, 2 * i:2 * i + 2, :, :].bitcast(F32), ALU.subtract).then_inc(free[BANK[f"yT{i}"]], 1)

            def mix0(n, _):
                if n.off > 0:
                    filled(dve, n + -1, "pv1")
                dve.wait_ge(p_delta, n.times(1, 1))
                for f in range(KD):
                    ins = nc.vector.scalar_tensor_tensor(mx[:, 0, f, :], delta[:, f, :], vec_s[:, NC_MU + f:NC_MU + f + 1],
                                                         xT[:, n.off % 2, f, 1:TB + 1], ALU.mult, ALU.add)
                ins.then_inc(v_mx0, 1)

            def split_z(n, _):
                emptied(dve, n, "z")
                nc.vector.tensor_tensor(z0_low[:, :], z0[:, :], z0_high[:, :].bitcast(F32), ALU.subtract).then_inc(v_zl, 1)
                nc.vector.scalar_tensor_tensor(zs[:, MIX_G, :], zs[:, MIX_G, :].bitcast(F32), low_z[:, 0:1], z1[:, :],
                                               ALU.mult, ALU.add).then_inc(v_zl, 1)

            def mix_times_delta(n, part):
                a, i = part // 2, part % 2
                if first(n) and MIXES[a] == MIX_V and i == 0:
                    centre_value_weight()
                    binarise()
                if i == 0:
                    if a == 0 and n.off > 0:
                        filled(dve, n + -1, "pg1")
                    if a == 1:
                        wait(dve, pe_r, n.times(1))
                    if a >= 2:
                        filled(dve, n, ("z", "pw", "pk")[a - 2])
                name = f"mu{a}{'ab'[i]}"
                w = filled(dve, n, name)
                nc.vector.tensor_tensor(mx[:, (1 + a) % MXRING, 2 * i:2 * i + 2, :], w[:, :].rearrange("p (f t) -> p f t", f=2),
                                        delta[:, 2 * i:2 * i + 2, :], ALU.mult).then_inc(free[BANK[name]], 1)

            def gate_mult(n, i):
                dve.wait_ge(a_th, n.times(2, i + 1))
                gt = gate[:, n.off % 2, 2 * i:2 * i + 2, :]
                nc.vector.scalar_tensor_tensor(gt, gt, 1.0, W[BANK[f"pg{i}"]][:, :].rearrange("p (m t) -> p m t", m=2), ALU.add, ALU.mult)\
                    .then_inc(free[BANK[f"pg{i}"]], 1)

            def scan(j, v):
                if v % VG == 0:
                    wait(dve, pe_red, j.times(VT, v // VG + 1 - VT))
                    if j.off % PER_SEQ == 0:
                        nc.vector.memset(state[:, v:v + VG, :, 0:1], 0.0).then_inc(v_c, 1)
                    else:
                        nc.vector.tensor_copy(state[:, v:v + VG, :, 0:1], state[:, v:v + VG, :, TB:TB + 1]).then_inc(v_c, 1)
                    dve.wait_ge(v_c, j.times(VT, v // VG + 1))
                if v == 0:
                    dve.wait_ge(a_d, j.times(1, 1))
                dve.wait_ge(p_kv, j.times(HV, v + 1))
                for hh in range(HH):
                    ins = nc.vector.tensor_tensor_scan(state[:, v, hh, 1:TB + 1], d_t[:, hh, :], kv[:, v % KVRING, hh, :],
                                                       state[:, v, hh, 0:1], ALU.mult, ALU.add)
                ins.then_inc(v_scan, 1)

            def products(j, v):
                dve.wait_ge(v_scan, j.times(HV, v + 1))
                if v == 0:
                    dve.wait_ge(pe_r, j.times(1, 1))
                nc.vector.tensor_tensor(state[:, v, :, 0:TB], state[:, v, :, 0:TB], r_t, ALU.mult).then_inc(v_p, 1)

            def bonus_product(j, _):
                emptied(dve, j, "pk")
                dve.wait_ge(pe_r, j.times(1, 1))
                for hh in range(HH):
                    ins = nc.vector.scalar_tensor_tensor(ruk[:, hh, :], r_t[:, hh, :], vec_s[:, NC_U + hh:NC_U + hh + 1],
                                                         kT[:, j.off % 2, hh, :], ALU.mult, ALU.mult)
                ins.then_inc(v_ruk, 1)

            def sum_o(j, i):
                dve.wait_ge(p_bv, j.times(1, 1))
                dve.wait_ge(pe_red, j.times(VT, 2 * i + 2))
                o = ob[:, j.off % 2, 2 * i:2 * i + 2, :]
                nc.vector.tensor_tensor(o, o, O[i][:, :].rearrange("p (m t) -> p m t", m=2), ALU.add).then_inc(v_ob, 1)

            def normalise(t, _):
                wait(dve, v_on, t.times(1))
                emptied(dve, t, "var")
                nc.vector.reciprocal(sdo[:, :], sdo[:, :]).then_inc(v_rg, 1)
                dve.wait_ge(v_rg, t.times(1, 1))
                o = ob[:, t.off % 2, :, :]
                nc.vector.tensor_tensor(o, o, sdo[:, :].rearrange("p (m t) -> p m t", m=1).to_broadcast([P, VT, TB]), ALU.mult)\
                    .then_inc(v_on, 1)

            whole_run(dve, {"dv_idx": clamp_idx, "dv_lora": add_lora, "dv_st1": stats1, "dv_signs": take_signs, "dv_r1": scale1, "dv_mix0": mix0,
                            "dv_zl": split_z, "dv_mus": mix_times_delta, "dv_gate": gate_mult, "dv_scan": scan, "dv_prod": products,
                            "dv_ruk": bonus_product, "dv_ob": sum_o, "dv_on": normalise,
                            "dv_h2": add_attention, "dv_st2": stats2, "dv_r2": scale2, "dv_yl": split_y, "dv_out": add_ffn})

        @block.tensor
        def _(pe):
            pe.wait_ge(w_first, 16 * 3)
            pe.wait_ge(c_k, 4)

            def turn_signs():
                pe.wait_ge(c_f, 3)
                for f in range(KD):
                    if f >= 2:
                        pe.wait_ge(c_fc, f - 1)
                    for o in range(KD):
                        ins = nc.tensor.transpose(O[f % 2][:, o * P:o * P + P], bw[:, o, f * P:f * P + P], ident[:, :])
                    ins.then_inc(c_ft, 1)

            def fill(b, name):
                wait(pe, free[BANK[name]], b.fill(name, -1))
                return W[BANK[name]], full[BANK[name]]

            def project(w, bank, src, m, cols=P):
                for k in range(KD):
                    ins = nc.tensor.matmul(bank, w[:, k, m * P:m * P + cols], src[:, k, :], start=(k == 0), stop=(k == KD - 1))
                return ins

            def turn(w, src, i):
                for g in range(2):
                    for c in range(TC):
                        ins = nc.tensor.transpose(w[:, (2 * g + c) * P:(2 * g + c + 1) * P],
                                                  src[:, c, (2 * i + g) * P:(2 * i + g + 1) * P], ident[:, :])
                return ins

            def lora_turn(n, _):
                q = n.off % 4
                wait(pe, rows_in[q], n.round(4, 64, 64))
                w, f = fill(n, "agT")
                nc.tensor.transpose(w[:, 0:P], ag[:, q % 2, :, :].rearrange("p c r -> p (c r)"), ident[:, :]).then_inc(f, 1)

            def lora(n, _):
                emptied(pe, n, "agT")
                banks = [fill(n, f"lora{c}") for c in range(TC)]
                for c, (w, f) in enumerate(banks):
                    r0 = P // TC * c
                    nc.tensor.matmul(w[:, :], agT[r0:r0 + RANK, :], bt_s[r0:r0 + RANK, :], start=True, stop=True,
                                     tile_position=(r0, 0)).then_inc(f, 1)

            def turn_x(n, i):
                pe.wait_ge(a_xn, n.times(1, 1))
                w, f = fill(n, f"xT{i}")
                turn(w, xn, i).then_inc(f, 1)

            def turn_y(t, i):
                pe.wait_ge(a_yn, t.times(1, 1))
                w, f = fill(t, f"yT{i}")
                turn(w, xn, i).then_inc(f, 1)

            def token_shift_rank(n, _):
                pe.wait_ge(v_mx0, n.times(1, 1))
                if first(n):
                    pe.wait_ge(w_x, 16 * (1 + P // RLO))
                w, f = fill(n, "z")
                project(wx1_s, w[:, 0:TB], mx[:, 0, :, :], 0)
                for k in range(KD):
                    for q in range(P // RLO):
                        ins = nc.tensor.matmul(w[q * RLO:(q + 1) * RLO, TB:2 * TB], wx1_s[:, k, P:P + RLO], mx[:, 0, k, :],
                                               start=(k == 0), stop=(k == KD - 1), tile_position=(0, q * RLO))
                ins.then_inc(f, 1)

            def spread_z(n, i):
                pe.wait_ge(v_zl, n.times(2, 1))
                if first(n) and i == 0:
                    pe.wait_ge(c_rank, 2)
                    pe.wait_ge(c_w, 2)
                w, f = fill(n, f"zr{i}")
                for g in range(2):
                    at = 2 + 4 * (2 * i + g)
                    nc.tensor.matmul(w[:, g * TB:g * TB + TB], rank_sel[:, at:at + 4, :].rearrange("p q r -> p (q r)"), z0_high[:, :],
                                     start=True, stop=False)
                    ins = nc.tensor.matmul(w[:, g * TB:g * TB + TB], rank_sel[:, at - 2:at + 2, :].rearrange("p q r -> p (q r)"), z0_low[:, :],
                                           start=False, stop=True)
                ins.then_inc(f, 1)

            def mus(n, a):
                m = MIXES[a]
                if m == MIX_G:
                    pe.wait_ge(v_zl, n.times(2, 2))
                else:
                    emptied(pe, n, f"zr{m // 2}")
                for i in range(2):
                    w, f = fill(n, f"mu{a}{'ab'[i]}")
                    for g in range(2):
                        f0 = (2 * i + g) * P
                        ins = nc.tensor.matmul(w[:, g * TB:g * TB + TB], wx2_s[:, m, f0:f0 + P], zs[:, m, :], start=True, stop=True)
                    ins.then_inc(f, 1)

            def mixed(n, a):
                pe.wait_ge(p_add, n.times(5, a + 1))
                return mx[:, (1 + a) % MXRING, :, :]

            def proj(n, a):
                if first(n):
                    pe.wait_ge(w_in, 16 * 6)
                src = mixed(n, a)
                if MIXES[a] == MIX_W:
                    w, f = fill(n, "pw")
                    project(ww1_s, w[0:GLO, 0:TB], src, 0, GLO).then_inc(f, 1)
                if MIXES[a] == MIX_K:
                    w, f = fill(n, "pk")
                    for hh in range(HH):
                        ins = project(wk_s, w[:, hh * TB:hh * TB + TB], src, hh)
                    ins.then_inc(f, 1)
                if MIXES[a] == MIX_R:
                    wait(pe, v_p, n.times(HV))
                    for hh in range(HH):
                        ins = project(wr_s, R[:, hh * TB:hh * TB + TB], src, hh)
                    ins.then_inc(pe_r, 1)

            def proj_v(n, i):
                src = mixed(n, MIXES.index(MIX_V))
                if first(n) and i == 0:
                    pe.wait_ge(c_v, 1 + KD)
                    turn_signs()
                w, f = fill(n, f"pv{i}")
                for g in range(2):
                    ins = project(wv_s, w[:, g * TB:g * TB + TB], src, 2 * i + g)
                ins.then_inc(f, 1)

            def proj_g(n, i):
                src = mixed(n, MIXES.index(MIX_G))
                if first(n) and i == 0:
                    pe.wait_ge(w_in, 16 * 6)
                w, f = fill(n, f"pg{i}")
                for g in range(2):
                    ins = project(wg_s, w[:, g * TB:g * TB + TB], src, 2 * i + g)
                ins.then_inc(f, 1)

            def decay_rank(n, _):
                emptied(pe, n, "pw")
                w, f = fill(n, "w2")
                for hh in range(HH):
                    ins = nc.tensor.matmul(w[:, hh * TB:hh * TB + TB], ww2_s[:, hh * P:hh * P + P], t2[:, :], start=True, stop=True)
                ins.then_inc(f, 1)

            def bonus_sum(j, _):
                pe.wait_ge(v_ruk, j.times(1, 1))
                w, f = fill(j, "bs")
                for hh in range(HH):
                    ins = nc.tensor.matmul(w[:, 0:TB], head_sel[:, hh, :, :].rearrange("p v h -> p (v h)"), ruk[:, hh, :],
                                           start=(hh == 0), stop=(hh == HH - 1))
                ins.then_inc(f, 1)

            def reduce_heads(j, m):
                if m % 2 == 0:
                    wait(pe, v_ob, j.times(2, m // 2 - 1))
                pe.wait_ge(v_p, j.times(HV, VG * (m + 1)))
                for hh in range(HH):
                    for vi in range(VG):
                        ins = nc.tensor.matmul(O[m // 2][NH * vi:NH * vi + NH, (m % 2) * TB:(m % 2) * TB + TB],
                                               head_sel[:, hh, 0, :], state[:, VG * m + vi, hh, 0:TB],
                                               start=(hh == 0), stop=(hh == HH - 1), tile_position=(0, NH * vi))
                ins.then_inc(pe_red, 1)

            def variance(t, _):
                pe.wait_ge(p_sq, t.times(2, 2))
                w, f = fill(t, "var")
                nc.tensor.matmul(w[:, 0:TB], head_mean[:, :, :].rearrange("p v h -> p (v h)"), sq[:, 0, :], start=True, stop=True).then_inc(f, 1)

            def proj_o(t, c):
                pe.wait_ge(p_y, t.times(1, 1))
                w, f = fill(t, f"wo{c}")
                for m in range(VT):
                    ins = nc.tensor.matmul(w[:, :], yT[:, m, c:TB:TC], wo_s[:, m, :], start=(m == 0), stop=(m == VT - 1))
                ins.then_inc(f, 1)

            def ffn(t, i):
                emptied(pe, t, "yT1")
                w, f = fill(t, f"f{i}")
                for g in range(2):
                    o = 2 * i + g
                    for k in range(KD):
                        for y in (y2T_high, y2T_low):
                            ins = nc.tensor.matmul(w[:, g * TB:g * TB + TB], wf_s[:, k, o * P:o * P + P],
                                                   y[:, k, :, :].rearrange("p c t -> p (c t)"),
                                                   start=(k == 0 and y is y2T_high), stop=(k == KD - 1 and y is y2T_low))
                ins.then_inc(f, 1)

            def turn_ffn(t, c):
                emptied(pe, t, "f1")
                w, f = fill(t, f"fT{c}")
                for o in range(KD):
                    ins = nc.tensor.transpose(w[:, o * P:o * P + P], fT[:, o, c * P:c * P + P], ident[:, :])
                ins.then_inc(f, 1)

            whole_run(pe, {"pe_agT": lora_turn, "pe_lora": lora, "pe_xT": turn_x, "pe_yT": turn_y, "pe_z": token_shift_rank,
                           "pe_zr": spread_z, "pe_mus": mus, "pe_proj": proj, "pe_pv": proj_v, "pe_pg": proj_g, "pe_w2": decay_rank,
                           "pe_bs": bonus_sum, "pe_red": reduce_heads, "pe_var": variance, "pe_wo": proj_o,
                           "pe_ffn": ffn, "pe_fT": turn_ffn})


_ORDER = ["x", "w_tok", "a_tok", "b_tok", "vecs", "wx1", "wx2", "wr", "ww1", "ww2", "wk", "wv", "wg", "wo", "w_ffn"]


def kernel(x, L0_tok_W, L0_tok_A, L0_tok_B, L0_attn_mu_x, L0_attn_Wx1, L0_attn_Wx2, L0_attn_Wr, L0_attn_Ww1, L0_attn_Ww2,
           L0_attn_bw, L0_attn_Wk, L0_attn_Wv, L0_attn_Wg, L0_attn_bonus, L0_attn_gn_w, L0_attn_gn_b, L0_attn_Wo,
           L0_ffn_weight, L0_ffn_bias):
    import numpy as np
    from concourse import bacc
    from concourse.bass_utils import run_bass_kernel_spmd

    def columns(v):
        return np.asarray(v).reshape(-1, P).T

    def value_major(w):
        return np.asarray(w).reshape(-1, NH, HV).transpose(0, 2, 1).reshape(-1, D)

    gn = [columns(np.repeat(np.asarray(v), NH)) for v in (L0_attn_gn_w, L0_attn_gn_b)]
    given = {
        "x": np.asarray(x).reshape(NBLK, P, TC),
        "w_tok": L0_tok_W, "a_tok": L0_tok_A, "b_tok": L0_tok_B,
        "vecs": np.concatenate([columns(L0_attn_mu_x), columns(L0_attn_bonus), columns(L0_attn_bw)] + gn + [columns(L0_ffn_bias)], axis=1),
        "wx1": L0_attn_Wx1, "wx2": np.asarray(L0_attn_Wx2).reshape(5 * RLO, D), "wr": L0_attn_Wr, "ww1": L0_attn_Ww1,
        "ww2": L0_attn_Ww2, "wk": L0_attn_Wk, "wv": value_major(L0_attn_Wv), "wg": value_major(L0_attn_Wg),
        "wo": value_major(np.asarray(L0_attn_Wo).T).T, "w_ffn": L0_ffn_weight,
    }
    nc = bacc.Bacc("TRN2", target_bir_lowering=False, num_devices=1, dynamic_dma_scratch_size=4096)
    arrays, args = {}, []
    for name in _ORDER:
        a = np.ascontiguousarray(given[name])
        arrays[f"in_{name}"] = a
        args.append(nc.dram_tensor(f"in_{name}", a.shape, mybir.dt.from_np(a.dtype), kind="ExternalInput").ap())
    args.append(nc.dram_tensor("out_h", (NBLK, P, TC * D), F32, kind="ExternalOutput").ap())
    tower_kernel(nc, *args)
    r = run_bass_kernel_spmd(nc, [arrays], core_ids=[0])
    return r.results[0]["out_h"].reshape(SEQS, SEQ, D)
```
